# Optimizing a Trainium2 kernel written in Bass

```python
import numpy as np
import jax
import jax.numpy as jnp

def _softmax(x, axis=-1):
    return jax.nn.softmax(x, axis=axis)
def _gelu(x):
    return jax.nn.gelu(x, approximate=True)
def _silu(x):
    return jax.nn.silu(x)
def _sigmoid(x):
    return jax.nn.sigmoid(x)
def _layernorm(x, axis=-1, eps=1e-5):
    m = jnp.mean(x, axis=axis, keepdims=True)
    v = jnp.var(x, axis=axis, keepdims=True)
    return (x - m) / jnp.sqrt(v + eps)
def _scatter_add(tgt, idx, src, axis=0):
    return tgt.at[idx].add(src)
def _segment_sum(src, seg, n):
    return jax.ops.segment_sum(src, seg, n)

kernel_name = 'mk_adj_preln_d1_adj_256_a09931'

def setup_inputs(seed: int = 0):
    np.random.seed(seed)
    _w = jnp.asarray
    def _rec_inputs():
        import jax
        import jax.numpy as jnp
        _gk = jax.random.key(seed)
        x = -0.0006008 + 1.001 * jax.random.normal(jax.random.fold_in(_gk, 1), (8192, 256), jnp.float32)
        _a = jax.random.bernoulli(jax.random.fold_in(_gk, 2), 0.000488281, (8192, 8192))
        adj = _a.astype(jnp.int32)
        return x, adj
    x, adj = _rec_inputs()
    def _L0_gnn_setup():
        import jax, jax.numpy as jnp
        import numpy as np
        N, D_IN, D_OUT = (10000, 256, 256)
        key = jax.random.key(seed)
        k1, k2, k3, k4 = jax.random.split(key, 4)

        def xavier(k, shape, gain=1.414):
            fan_in, fan_out = (shape[0], shape[1])
            bound = gain * np.sqrt(6.0 / (fan_in + fan_out))
            return jax.random.uniform(k, shape, jnp.float32, -bound, bound)
        return {'input': jax.random.normal(k1, (N, D_IN), jnp.float32), 'adj': jax.random.randint(k2, (N, N), 0, 2, jnp.int32), 'M': N, 'W': xavier(k3, (D_IN, D_OUT)), 'b': jnp.zeros((D_OUT,), jnp.float32), 'a': xavier(k4, (D_OUT, 1))}
    _L0_gnn_all = _L0_gnn_setup()
    _L0_gnn_in = {k: v for k, v in _L0_gnn_all.items() if k in ('W', 'b', 'a', )}
    del _L0_gnn_all

    return {
        "x": x,
        "adj": adj,
        "L0_gnn_W": _L0_gnn_in["W"],
        "L0_gnn_b": _L0_gnn_in["b"],
        "L0_gnn_a": _L0_gnn_in["a"],
    }

def reference(x, adj, L0_gnn_W, L0_gnn_b, L0_gnn_a):
    import jax
    import jax.numpy as jnp
    def _L0_gnn_ref(input, adj, M, W, b, a):
        import jax, jax.numpy as jnp
        import numpy as np
        N, D_IN, D_OUT = (10000, 256, 256)
        h = jnp.tanh(input @ W + b)
        inp = input @ W
        e = (h @ a)[:, 0]
        valid = jnp.sum(h, axis=1) != 0
        mask = (adj[:M] > 0) & valid[None, :]
        neg = jnp.asarray(-1e+30, h.dtype)
        scores = jnp.where(mask, e[None, :], neg)
        m = jnp.max(scores, axis=1, keepdims=True)
        w = jnp.where(mask, jnp.exp(scores - m), 0.0)
        denom = jnp.sum(w, axis=1, keepdims=True)
        att = w / jnp.maximum(denom, 1e-30)
        return att @ inp

    h = jnp.maximum(_layernorm(x, axis=-1), 0.0)
    x = x + _L0_gnn_ref(h, adj, 8192, L0_gnn_W, L0_gnn_b, L0_gnn_a)
    return x


_drawn_inputs = setup_inputs


def setup_inputs(seed=0):
    import zlib

    import numpy as np

    out = dict(_drawn_inputs(seed))
    spreads = {'L0_gnn_b': (0.0, 0.547)}
    factors = {}
    for name, (base, spread) in spreads.items():
        noise = np.random.default_rng([zlib.crc32(name.encode()), seed]).standard_normal(out[name].shape)
        drawn = base * np.exp(spread * noise) if base else spread * noise
        out[name] = jnp.asarray(drawn.astype(out[name].dtype))
    for name, factor in factors.items():
        out[name] = (out[name] * factor).astype(out[name].dtype)
    return out
```

```python
import concourse.bass as bass
from concourse import mybir
from contextlib import ExitStack


def gnn_layer(nc: bass.Bass, x: bass.AP, adj: bass.AP, W: bass.AP, b: bass.AP, a: bass.AP, out: bass.AP):
    f32, bf16, i32, u32 = mybir.dt.float32, mybir.dt.bfloat16, mybir.dt.int32, mybir.dt.uint32
    ALU, ACT, AX = mybir.AluOpType, mybir.ActivationFunctionType, mybir.AxisListType

    P = 128
    N, D = x.shape
    T = N // P
    DK = D // P
    HALF = N // 2
    NBLK = 8
    BW = N // NBLK
    BANK = 512
    NB = BW // BANK
    NCH = 4
    CW = BW // NCH
    NF = NCH * 8
    K = 16
    TW = D + 1
    NEG = -1e30
    EPS = 1e-5
    BATCH = 16
    NBATCH = T // BATCH
    QUAD = 4
    LAG = 2 * NBATCH
    GB = 8
    EXPMASK, MANT, EBIAS = 0x7F800000, 23, 127

    table = nc.dram_tensor("table", (N, TW), f32, kind="Internal").ap()
    erow = nc.dram_tensor("erow", (T, P), f32, kind="Internal").ap()
    x_b = x.rearrange("(n i p) d -> n p i d", p=P, i=BATCH)
    x_t = x.rearrange("(t p) d -> t p d", p=P)
    out_t = out.rearrange("(t p) d -> t p d", p=P)
    adj_t = adj.rearrange("(t p) (h c) -> t h p c", p=P, h=2)
    table_q = table.rearrange("(q i p) c -> q p i c", p=P, i=QUAD)
    table_g = table.rearrange("(g i p) c -> g p i c", p=P, i=GB)

    with ExitStack() as ctx:
        def sb(name, shape, dt):
            return ctx.enter_context(nc.sbuf_tensor(name, shape, dt))

        def ps(name, shape, dt=f32):
            return ctx.enter_context(nc.psum_tensor(name, shape, dt))

        def sem(name):
            return ctx.enter_context(nc.semaphore(name))

        ident = sb("ident", [P, P], f32)
        shifts = sb("shifts", [P, NBLK, P], bf16)
        ones = sb("ones", [P, P], f32)
        base = sb("base", [P, NCH, 8], f32)
        w_sb = sb("w_sb", [P, DK, D], f32)
        bias = sb("bias", [P, D], f32)
        avec = sb("avec", [P, D], f32)
        adj_sb = sb("adj_sb", [P, 2, 2, HALF], i32)
        mask = sb("mask", [P, 2, 2, HALF], bf16)
        halfdeg = sb("halfdeg", [P, 2, T], f32)
        deg = sb("deg", [P, T], f32)
        found = sb("found", [P, T], f32)
        vals = sb("vals", [P, 2, NF], f32)
        pos = sb("pos", [P, NF], u32)
        expo = sb("expo", [P, 2, NF], i32)
        col = sb("col", [P, NF], f32)
        key = sb("key", [P, 2, NF], f32)
        key2 = sb("key2", [P, 2 * NF], f32)
        top = sb("top", [P, K], f32)
        junk16 = sb("junk16", [P, K], f32)
        keys = sb("keys", [P, T, K], f32)
        slots = sb("slots", [P, 2, K, TW], f32)
        idx = sb("idx", [P, 2, K], u32)
        pen = sb("pen", [P, 2, K], f32)
        sc = sb("sc", [P, 2, K], f32)
        rmax = sb("rmax", [P, 2, 1], f32)
        nmax = sb("nmax", [P, 2, 1], f32)
        wt = sb("wt", [P, 2, K], f32)
        den = sb("den", [P, 2, 1], f32)
        dmax = sb("dmax", [P, 2, 1], f32)
        rden = sb("rden", [P, 2, 1], f32)
        diag = sb("diag", [P, 2, K, P], f32)
        xt = sb("xt", [P, 2, D], f32)
        ot = sb("ot", [P, 2, D], f32)
        stats = sb("stats", [P, BATCH, 6], f32)
        msum = sb("msum", [P, BATCH], f32)
        mdif = sb("mdif", [P, BATCH], f32)
        var = sb("var", [P, BATCH], f32)
        std = sb("std", [P, BATCH], f32)
        rstd = sb("rstd", [P, BATCH], f32)
        nmr = sb("nmr", [P, BATCH], f32)
        h = sb("h", [P, 2, D], f32)
        hT = sb("hT", [P, 2, D], f32)
        zb = sb("zb", [P, 2, D], f32)
        th = sb("th", [P, 2, D], f32)
        junk = sb("junk", [P, D], f32)
        stage = sb("stage", [P, 2, QUAD, TW], f32)
        hsum = sb("hsum", [P, 2, QUAD], f32)
        escore = sb("escore", [P, 2, QUAD], f32)
        epen = sb("epen", [P, 2, QUAD], f32)
        escores = sb("escores", [P, T], f32)
        lost = sb("lost", [P, T], f32)
        tord = sb("tord", [1, T], f32)
        tflag = sb("tflag", [1, T], f32)
        tkey = sb("tkey", [1, T], f32)
        tlist = sb("tlist", [1, T], f32)
        tiles = sb("tiles", [1, T], i32)
        nflag = sb("nflag", [1, 1], f32)
        ntiles = sb("ntiles", [1, 1], i32)
        eT = sb("eT", [T, P], f32)

        packed = [[ps(f"packed{p}{n}", [P, BANK]) for n in range(NB)] for p in range(2)]
        pT = [ps(f"pT{p}", [P, D]) for p in range(2)]
        pz = [ps(f"pz{p}", [P, D]) for p in range(2)]
        acc = pT

        consts = sem("consts")
        gconst = sem("gconst")
        params_in = sem("params_in")
        x_in = [sem(f"x_in{p}") for p in range(2)]
        var_ready = sem("var_ready")
        std_ready = sem("std_ready")
        rstd_ready = sem("rstd_ready")
        h_ready = [sem(f"h_ready{p}") for p in range(2)]
        hT_psum = [sem(f"hT_psum{p}") for p in range(2)]
        hT_ready = [sem(f"hT_ready{p}") for p in range(2)]
        z_psum = [sem(f"z_psum{p}") for p in range(2)]
        z_staged = [sem(f"z_staged{p}") for p in range(2)]
        zb_ready = [sem(f"zb_ready{p}") for p in range(2)]
        th_ready = [sem(f"th_ready{p}") for p in range(2)]
        dotted = [sem(f"dotted{p}") for p in range(2)]
        staged = sem("staged")
        stored = sem("stored")
        stage_free = [sem(f"stage_free{p}") for p in range(2)]
        adj_in = [[sem(f"adj_in{p}{i}") for i in range(2)] for p in range(2)]
        adj_free = [[sem(f"adj_free{p}{i}") for i in range(2)] for p in range(2)]
        mask_free = [[sem(f"mask_free{p}{i}") for i in range(2)] for p in range(2)]
        packed_free = [sem(f"packed_free{p}") for p in range(2)]
        idx_ready = [sem(f"idx_ready{p}") for p in range(2)]
        gathering = [sem(f"gathering{p}") for p in range(2)]
        gathered = [sem(f"gathered{p}") for p in range(2)]
        sc_ready = [sem(f"sc_ready{p}") for p in range(2)]
        wt_ready = [sem(f"wt_ready{p}") for p in range(2)]
        diag_ready = [sem(f"diag_ready{p}") for p in range(2)]
        acc_ready = [sem(f"acc_ready{p}") for p in range(2)]
        xt_in = [sem(f"xt_in{p}") for p in range(2)]
        ot_ready = [sem(f"ot_ready{p}") for p in range(2)]
        ot_out = [sem(f"ot_out{p}") for p in range(2)]
        lost_ready = sem("lost_ready")
        lost_psum = sem("lost_psum")
        list_ready = sem("list_ready")
        et_psum = sem("et_psum")
        et_ready = sem("et_ready")
        erow_out = sem("erow_out")
        g_adj = sem("g_adj")
        g_e = sem("g_e")
        g_x = sem("g_x")
        g_table = [sem(f"g_table{p}") for p in range(2)]
        g_nmax = sem("g_nmax")
        g_w = sem("g_w")
        g_tr = [sem(f"g_tr{p}") for p in range(2)]
        g_wT = [sem(f"g_wT{p}") for p in range(2)]
        g_mm = [sem(f"g_mm{p}") for p in range(2)]
        g_acc = sem("g_acc")
        g_ot = sem("g_ot")
        g_out = sem("g_out")
        g_stored = sem("g_stored")

        g_mask_i = adj_sb[:, 0, :, :].rearrange("p h c -> p (h c)")
        g_mask_f = g_mask_i.bitcast(f32)
        g_w_f = adj_sb[:, 1, :, :].rearrange("p h c -> p (h c)").bitcast(f32)
        g_tab = [slots[:, p, 0:GB, :] for p in range(2)]
        g_wTs = [diag[:, p, 0:4, :].rearrange("p k c -> p (k c)") for p in range(2)]
        NG = T // GB
        NQ = T // 4

        NCONST = 5 + NBLK

        block = ctx.enter_context(nc.Block())

        def steps(engine, step):
            step(0, 0, first=True)
            step(0, 1)
            step(1, 0)
            step(1, 1)
            with engine.Fori(2, (T - LAG) // 2) as k:
                step(k, 0)
                step(k, 1)
            with engine.Fori((T - LAG) // 2, T // 2 - 1) as k:
                step(k, 0, scan_too=False)
                step(k, 1, scan_too=False)
            step(T // 2 - 1, 0, scan_too=False)
            step(T // 2 - 1, 1, scan_too=False, last=True)

        def free(m):
            return m + 1

        def ready(m):
            return m + 2

        def after(k, par):
            return (k, 1) if par == 0 else (k + 1, 0)

        def before(k, par):
            return (k, 0) if par == 1 else (k - 1, 1)

        @block.sync
        def _(sp):
            sp.dma_start(w_sb[:, :, :], W.rearrange("(k p) d -> p k d", p=P)).then_inc(params_in, 16)
            sp.dma_start(bias[:, :], b.partition_broadcast(P)).then_inc(params_in, 16)
            sp.dma_start(avec[:, :], a.rearrange("d o -> (o d)").partition_broadcast(P)).then_inc(params_in, 16)
            with sp.Fori(0, T // 2) as k:
                for par in range(2):
                    for i in range(2):
                        sp.wait_ge(adj_free[par][i], free(k))
                        sp.dma_start(adj_sb[:, par, i, :],
                                     adj_t[bass.ds(2 * k + par, 1), i, :, :].rearrange("o p c -> (o p) c"))\
                          .then_inc(adj_in[par][i], 16)

            sp.wait_ge(list_ready, 1)
            count = sp.value_load(ntiles[0:1, 0:1], min_val=0, max_val=T)
            with sp.If(count > 0):
                for par in range(2):
                    sp.wait_ge(ot_out[par], 16 * (T // 2))
                sp.wait_ge(et_ready, 1)
                sp.dma_start(erow[:, :], eT[:, :]).then_inc(erow_out, 16)
                sp.wait_ge(erow_out, 16)
                sp.sem_inc(g_stored, 1)
                with sp.Fori(0, count) as r:
                    tile = sp.value_load(tiles[0:1, bass.ds(r, 1)], min_val=0, max_val=T - 1)
                    sp.wait_ge(g_stored, free(r))
                    sp.dma_start(g_mask_i, adj[bass.ds(tile * P, P), :]).then_inc(g_adj, 16)
                    sp.dma_start(g_w_f, erow.rearrange("t p -> (t p)").partition_broadcast(P)).then_inc(g_e, 16)
                    sp.dma_start(xt[:, 0, :], x[bass.ds(tile * P, P), :]).then_inc(g_x, 16)
                    for g in range(NG):
                        if g >= 2:
                            sp.wait_ge(g_mm[1], NQ // 2 * r + g - 1)
                        sp.dma_start(g_tab[g % 2], table_g[g]).then_inc(g_table[g % 2], 16)
                    sp.wait_ge(g_ot, r + 1)
                    sp.dma_start(out[bass.ds(tile * P, P), :], ot[:, 0, :]).then_inc(g_out, 16)
                    sp.wait_ge(g_out, 16 * (r + 1))
                    sp.sem_inc(g_stored, 1)

        @block.gpsimd
        def _(pool):
            for q in range(2):
                pool.sem_inc(stage_free[q], 1)
            nc.gpsimd.memset(ident[:, :], 0.0).then_inc(gconst, 1)
            nc.gpsimd.memset(shifts[:, :, :], 0.0).then_inc(gconst, 1)
            nc.gpsimd.memset(slots[:, :, :, D:TW], 0.0).then_inc(consts, 1)
            for par in range(2):
                pool.dma_start(slots[:, par, :, 0:D], x_b[par]).then_inc(x_in[par], 16)
            nc.gpsimd.memset(ones[:, :], 1.0).then_inc(consts, 1)
            nc.gpsimd.iota(base[:, :, :], pattern=[[-CW, NCH], [0, 8]], base=N + EBIAS * BW,
                           channel_multiplier=0, allow_small_or_imprecise_dtypes=True).then_inc(consts, 1)
            nc.gpsimd.iota(tord[:, :], pattern=[[-1, T]], base=T, channel_multiplier=0,
                           allow_small_or_imprecise_dtypes=True).then_inc(consts, 1)
            pool.wait_ge(gconst, 2)
            nc.gpsimd.affine_select(out=ident[:, :], in_=ident[:, :], compare_op=ALU.not_equal, fill=1.0,
                                    base=0, pattern=[[-1, P]], channel_multiplier=1).then_inc(consts, 1)
            for j in range(NBLK):
                nc.gpsimd.affine_select(out=shifts[:, j, :], in_=shifts[:, j, :], compare_op=ALU.not_equal,
                                        fill=float(2 ** j), base=0, pattern=[[-1, P]],
                                        channel_multiplier=1).then_inc(consts, 1)
            for n in range(NBATCH):
                for q in range(BATCH // QUAD):
                    g = n * (BATCH // QUAD) + q
                    pool.wait_ge(staged, g + 1)
                    pool.dma_start(table_q[g], stage[:, g % 2, :, :]).then_inc(stored, 16)
                    pool.wait_ge(stored, 16 * (g + 1))
                    pool.sem_inc(stage_free[g % 2], 1)
                if n + 2 < NBATCH:
                    for u in range(2):
                        pool.wait_ge(h_ready[u], ready(BATCH // 2 * (n + 1) - 1))
                    pool.dma_start(slots[:, n % 2, :, 0:D], x_b[n + 2]).then_inc(x_in[n % 2], 16)

            last_row = pool.alloc_register("last_row")
            pool.reg_mov(last_row, N - 1)

            def gather(k, par):
                pool.wait_ge(idx_ready[par], k + 1)
                pool.wait_ge(acc_ready[par], free(k))
                pool.sem_inc(gathering[par], 1)

                def fetch(s):
                    pool.indirect_dma_start(
                        out=slots[:, par, s, :], out_offset=None, in_=table[:, :],
                        in_offset=bass.IndirectOffsetOnAxis(ap=idx[:, par, s:s + 1], axis=0),
                        bounds_check=last_row, oob_is_err=False).then_inc(gathered[par], 16)

                for s in range(K):
                    fetch(s)

            with pool.Fori(0, T // 2) as k:
                gather(k, 0)
                gather(k, 1)

        @block.scalar
        def _(act):
            for par in range(2):
                for i in range(2):
                    act.sem_inc(adj_free[par][i], 1)

            def scan(k, par):
                for i in range(2):
                    act.wait_ge(adj_in[par][i], 16 * (k + 1))
                    act.wait_ge(mask_free[par][i], free(k))
                    nc.scalar.activation(mask[:, par, i, :], adj_sb[:, par, i, :], ACT.Relu,
                                         accum_out=halfdeg[:, i, bass.ds(2 * k + par, 1)])\
                      .then_inc(adj_free[par][i], 1)

            def relu(d, bp, hf, j):
                m, u = 4 * (4 * d + 2 * bp + hf) + j // 2, j % 2
                act.wait_ge(hT_psum[u], free(m))
                i = 8 * hf + j
                nc.scalar.activation(h[:, u, :], slots[:, bp, bass.ds(i, 1), 0:D].rearrange("p o d -> p (o d)"),
                                     ACT.Relu, scale=rstd[:, bass.ds(i, 1)],
                                     bias=nmr[:, bass.ds(i, 1)]).then_inc(h_ready[u], 1)

            def stage_z(d, bp, hf, j):
                m, u, q = 4 * (4 * d + 2 * bp + hf) + j // 2, j % 2, j // 4
                act.wait_ge(z_psum[u], ready(m))
                if j % 4 == 0:
                    act.wait_ge(stage_free[q], free(4 * d + 2 * bp + hf))
                nc.scalar.copy(stage[:, q, j % 4, 0:D], pz[u][:, :]).then_inc(z_staged[u], 1)

            def tanh(d, bp, hf, j):
                m, u, q = 4 * (4 * d + 2 * bp + hf) + j // 2, j % 2, j // 4
                act.wait_ge(zb_ready[u], ready(m))
                act.wait_ge(dotted[u], free(m))
                nc.scalar.activation(th[:, u, :], zb[:, u, :], ACT.Tanh,
                                     accum_out=hsum[:, q, j % 4:j % 4 + 1]).then_inc(th_ready[u], 1)

            for u in range(2):
                act.sem_inc(h_ready[u], 1)
                act.sem_inc(z_staged[u], 1)
                act.sem_inc(th_ready[u], 1)
            with act.Fori(0, NBATCH // 2) as d:
                for bp in range(2):
                    act.wait_ge(var_ready, 2 * d + bp + 1)
                    nc.scalar.activation(std[:, :], var[:, :], ACT.Sqrt).then_inc(std_ready, 1)
                    act.wait_ge(rstd_ready, 2 * d + bp + 1)
                    with act.Fori(0, 2) as hf:
                        relu(d, bp, hf, 0)
                        relu(d, bp, hf, 1)
                        for j in range(8):
                            stage_z(d, bp, hf, j)
                            if j + 2 < 8:
                                relu(d, bp, hf, j + 2)
                            tanh(d, bp, hf, j)
                    scan(2 * d + bp, 0)
                    scan(2 * d + bp, 1)

            def exps(k, par):
                act.wait_ge(sc_ready[par], k + 1)
                nc.scalar.activation(wt[:, par, :], sc[:, par, :], ACT.Exp, bias=nmax[:, par, :],
                                     accum_out=den[:, par, :]).then_inc(wt_ready[par], 1)

            def load_x(k, par):
                act.wait_ge(ot_ready[par], free(k))
                act.dma_start(xt[:, par, :], x_t[bass.ds(2 * k + par, 1), :, :].rearrange("o p d -> (o p) d"))\
                   .then_inc(xt_in[par], 16)

            def store(k, par):
                act.wait_ge(ot_ready[par], ready(k))
                act.dma_start(out_t[bass.ds(2 * k + par, 1), :, :].rearrange("o p d -> (o p) d"), ot[:, par, :])\
                   .then_inc(ot_out[par], 16)

            def step(k, par, first=False, scan_too=True, last=False):
                load_x(k, par)
                if scan_too:
                    scan(k + LAG // 2, par)
                exps(k, par)
                if not first:
                    store(*before(k, par))
                if last:
                    store(k, par)

            steps(act, step)
            for par in range(2):
                act.wait_ge(ot_out[par], 16 * (T // 2))

            act.wait_ge(list_ready, 1)
            count = act.value_load(ntiles[0:1, 0:1], min_val=0, max_val=T)
            with act.If(count > 0):
                with act.Fori(0, count) as r:
                    act.wait_ge(g_nmax, r + 1)
                    nc.scalar.activation(g_w_f, g_w_f, ACT.Exp, bias=nmax[:, 0, :],
                                         accum_out=den[:, 0, :]).then_inc(g_w, 1)

        @block.tensor
        def _(pe):
            for par in range(2):
                pe.sem_inc(hT_psum[par], 1)
                pe.sem_inc(z_psum[par], 1)
                pe.sem_inc(acc_ready[par], 1)
                for i in range(2):
                    pe.sem_inc(mask_free[par][i], 1)
            pe.wait_ge(consts, NCONST)
            pe.wait_ge(params_in, 48)

            def pack(k, par):
                for i in range(2):
                    pe.wait_ge(adj_free[par][i], ready(k))
                    if i == 0:
                        pe.wait_ge(packed_free[par], free(k))
                    for j in range(NBLK // 2):
                        for n in range(NB):
                            last = nc.tensor.matmul(packed[par][n][:, :], shifts[:, i * NBLK // 2 + j, :],
                                                    mask[:, par, i, j * BW + n * BANK:j * BW + (n + 1) * BANK],
                                                    start=(i == 0 and j == 0), stop=(i == 1 and j == NBLK // 2 - 1))
                    last.then_inc(mask_free[par][i], 1)

            def turn(d, bp, hf, j):
                m, u = 4 * (4 * d + 2 * bp + hf) + j // 2, j % 2
                pe.wait_ge(h_ready[u], ready(m))
                pe.wait_ge(hT_ready[u], free(m))
                for c in range(DK):
                    last = nc.tensor.transpose(pT[u][:, c * P:(c + 1) * P], h[:, u, c * P:(c + 1) * P], ident[:, :])
                last.then_inc(hT_psum[u], 1)

            def project(d, bp, hf, j):
                m, u = 4 * (4 * d + 2 * bp + hf) + j // 2, j % 2
                pe.wait_ge(hT_ready[u], ready(m))
                pe.wait_ge(z_staged[u], free(m))
                for c in range(DK):
                    last = nc.tensor.matmul(pz[u][:, :], hT[:, u, c * P:(c + 1) * P], w_sb[:, c, :],
                                            start=(c == 0), stop=(c == DK - 1))
                last.then_inc(z_psum[u], 1)

            with pe.Fori(0, NBATCH // 2) as d:
                for bp in range(2):
                    with pe.Fori(0, 2) as hf:
                        turn(d, bp, hf, 0)
                        for j in range(8):
                            if j + 1 < 8:
                                turn(d, bp, hf, j + 1)
                            project(d, bp, hf, j)
                    pack(2 * d + bp, 0)
                    pack(2 * d + bp, 1)
            for u in range(2):
                pe.wait_ge(z_staged[u], ready(T // 2 - 1))

            def sum_slots(k, par):
                pe.wait_ge(diag_ready[par], k + 1)
                pe.wait_ge(ot_ready[par], free(k))
                for s in range(K):
                    last = nc.tensor.matmul(acc[par][:, :], diag[:, par, s, :], slots[:, par, s, 0:D],
                                            start=(s == 0), stop=(s == K - 1))
                last.then_inc(acc_ready[par], 1)

            def step(k, par, first=False, scan_too=True, last=False):
                if scan_too:
                    pack(k + LAG // 2, par)
                sum_slots(k, par)

            steps(pe, step)

            pe.wait_ge(lost_ready, 1)
            nc.tensor.matmul(pT[0][:, 0:T], ones[:, :], lost[:, :], start=True, stop=True).then_inc(lost_psum, 1)

            pe.wait_ge(list_ready, 1)
            count = pe.value_load(ntiles[0:1, 0:1], min_val=0, max_val=T)
            with pe.If(count > 0):
                nc.tensor.transpose(pz[0][0:T, 0:P], escores[:, :], ident[:, :]).then_inc(et_psum, 1)
                with pe.Fori(0, count) as r:
                    def products(q):
                        pe.wait_ge(g_wT[q % 2], NQ // 2 * r + q // 2 + 1)
                        g = q // 2
                        pe.wait_ge(g_table[g % 2], 16 * (NG // 2 * r + g // 2 + 1))
                        for c in range(4):
                            last = nc.tensor.matmul(acc[0][:, :], g_wTs[q % 2][:, c * P:(c + 1) * P],
                                                    g_tab[g % 2][:, 4 * (q % 2) + c, 0:D],
                                                    start=(q == 0 and c == 0), stop=(q == NQ - 1 and c == 3))
                        last.then_inc(g_mm[q % 2], 1)
                        return last

                    pe.wait_ge(g_w, r + 1)
                    for q in range(NQ):
                        if q >= 2:
                            pe.wait_ge(g_wT[q % 2], NQ // 2 * r + q // 2)
                        for c in range(4):
                            last = nc.tensor.transpose(packed[q % 2][0][:, c * P:(c + 1) * P],
                                                       g_w_f[:, (4 * q + c) * P:(4 * q + c + 1) * P], ident[:, :])
                        last.then_inc(g_tr[q % 2], 1)
                        if q >= 1:
                            products(q - 1)
                    products(NQ - 1)

        @block.vector
        def _(dve):
            for par in range(2):
                dve.sem_inc(packed_free[par], 1)
                dve.sem_inc(hT_ready[par], 1)
                dve.sem_inc(zb_ready[par], 1)
                dve.sem_inc(dotted[par], 1)
                dve.sem_inc(ot_ready[par], 1)
            dve.wait_ge(consts, NCONST)
            dve.wait_ge(params_in, 48)

            def scan(k, par):
                v = nc.vector
                dve.wait_ge(mask_free[par][1], ready(k))
                v.tensor_tensor(deg[:, bass.ds(2 * k + par, 1)], halfdeg[:, 0, bass.ds(2 * k + par, 1)],
                                halfdeg[:, 1, bass.ds(2 * k + par, 1)], op=ALU.add)
                chunks = [packed[par][c * CW // BANK][:, c * CW % BANK:c * CW % BANK + CW] for c in range(NCH)]
                for c in range(NCH):
                    v.max(out=vals[:, 0, 8 * c:8 * c + 8], in_=chunks[c])
                v.drain()
                for c in range(NCH):
                    last = v.max_index(out=pos[:, 8 * c:8 * c + 8], in_max=vals[:, 0, 8 * c:8 * c + 8],
                                       in_values=chunks[c])
                last.then_inc(packed_free[par], 1)
                v.tensor_single_scalar(expo[:, 0, :], vals[:, 0, :].bitcast(i32), EXPMASK, op=ALU.bitwise_and)
                v.drain()
                v.tensor_tensor(vals[:, 1, :], vals[:, 0, :], expo[:, 0, :].bitcast(f32), op=ALU.subtract)
                v.tensor_tensor(col[:, :], base[:, :, :].rearrange("p c e -> p (c e)"), pos[:, :], op=ALU.subtract)
                v.drain()
                v.tensor_single_scalar(expo[:, :, :], vals[:, :, :].bitcast(i32), MANT, op=ALU.logical_shift_right)
                v.drain()
                for o in range(2):
                    v.scalar_tensor_tensor(key[:, o, :], in0=expo[:, o, :], scalar=-float(BW), in1=col[:, :],
                                           op0=ALU.mult, op1=ALU.add)
                v.drain()
                v.scalar_tensor_tensor(key2[:, :], in0=vals[:, :, :].rearrange("p o f -> p (o f)"), scalar=0.0,
                                       in1=key[:, :, :].rearrange("p o f -> p (o f)"), op0=ALU.is_gt, op1=ALU.mult)
                v.drain()
                v.max(out=top[:, 0:8], in_=key2[:, :])
                v.drain()
                v.match_replace(out=key2[:, :], in_to_replace=top[:, 0:8], in_values=key2[:, :], imm_value=0.0)
                v.drain()
                v.max(out=top[:, 8:16], in_=key2[:, :])
                v.drain()
                v.tensor_scalar(junk16[:, :], top[:, :], 0.0, None, op0=ALU.is_gt, op1=ALU.add,
                                accum_out=found[:, bass.ds(2 * k + par, 1)])
                v.tensor_scalar(keys[:, bass.ds(2 * k + par, 1), :].rearrange("p o s -> p (o s)"), top[:, :],
                                1.0, None, op0=ALU.mult)
                v.drain()

            def copy_hT(d, bp, hf, j):
                m, u = 4 * (4 * d + 2 * bp + hf) + j // 2, j % 2
                dve.wait_ge(hT_psum[u], ready(m))
                dve.wait_ge(z_psum[u], free(m))
                nc.vector.tensor_copy(hT[:, u, :], pT[u][:, :]).then_inc(hT_ready[u], 1)

            def add_bias(d, bp, hf, j):
                m, u, q = 4 * (4 * d + 2 * bp + hf) + j // 2, j % 2, j // 4
                dve.wait_ge(z_staged[u], ready(m))
                dve.wait_ge(th_ready[u], free(m))
                nc.vector.tensor_tensor(zb[:, u, :], stage[:, q, j % 4, 0:D], bias[:, :],
                                        op=ALU.add).then_inc(zb_ready[u], 1)

            def dot_a(d, bp, hf, j):
                m, u, q = 4 * (4 * d + 2 * bp + hf) + j // 2, j % 2, j // 4
                dve.wait_ge(th_ready[u], ready(m))
                nc.vector.scalar_tensor_tensor(junk[:, :], in0=th[:, u, :], scalar=1.0, in1=avec[:, :],
                                               op0=ALU.mult, op1=ALU.mult,
                                               accum_out=escore[:, q, j % 4:j % 4 + 1]).then_inc(dotted[u], 1)

            def scores(d, bp, hf, q):
                nc.vector.drain()
                nc.vector.tensor_scalar(epen[:, q, :], hsum[:, q, :], 0.0, NEG, op0=ALU.is_equal, op1=ALU.mult)
                nc.vector.drain()
                g = 2 * (4 * d + 2 * bp + hf) + q
                nc.vector.tensor_tensor(escores[:, bass.ds(QUAD * g, QUAD)], escore[:, q, :], epen[:, q, :], op=ALU.add)
                nc.vector.tensor_tensor(stage[:, q, :, D], escore[:, q, :], epen[:, q, :],
                                        op=ALU.add).then_inc(staged, 1)

            with dve.Fori(0, NBATCH // 2) as d:
                for bp in range(2):
                    v = nc.vector
                    with dve.Fori(0, BATCH) as i:
                        dve.wait_ge(x_in[bp], 16 * (d + 1))
                        v.bn_stats(out=stats[:, bass.ds(i, 1), :].rearrange("p o s -> p (o s)"),
                                   in_=slots[:, bp, bass.ds(i, 1), 0:D].rearrange("p o d -> p (o d)"))
                    v.drain()
                    v.tensor_tensor(msum[:, :], stats[:, :, 1], stats[:, :, 4], op=ALU.add)
                    v.tensor_tensor(mdif[:, :], stats[:, :, 1], stats[:, :, 4], op=ALU.subtract)
                    v.tensor_tensor(var[:, :], stats[:, :, 2], stats[:, :, 5], op=ALU.add)
                    v.drain()
                    v.scalar_tensor_tensor(mdif[:, :], in0=mdif[:, :], scalar=0.25, in1=mdif[:, :],
                                           op0=ALU.mult, op1=ALU.mult)
                    v.tensor_scalar(var[:, :], var[:, :], 1.0 / D, EPS, op0=ALU.mult, op1=ALU.add)
                    v.drain()
                    v.tensor_tensor(var[:, :], var[:, :], mdif[:, :], op=ALU.add).then_inc(var_ready, 1)
                    dve.wait_ge(std_ready, 2 * d + bp + 1)
                    v.reciprocal(rstd[:, :], std[:, :])
                    v.drain()
                    v.scalar_tensor_tensor(nmr[:, :], in0=msum[:, :], scalar=-0.5, in1=rstd[:, :],
                                           op0=ALU.mult, op1=ALU.mult).then_inc(rstd_ready, 1)
                    with dve.Fori(0, 2) as hf:
                        copy_hT(d, bp, hf, 0)
                        copy_hT(d, bp, hf, 1)
                        for j in range(8):
                            add_bias(d, bp, hf, j)
                            if j + 2 < 8:
                                copy_hT(d, bp, hf, j + 2)
                            dot_a(d, bp, hf, j)
                            if j % 4 == 3:
                                scores(d, bp, hf, j // 4)
                    scan(2 * d + bp, 0)
                    scan(2 * d + bp, 1)

            def issue(k, par):
                n = 2 * k + par
                nc.vector.tensor_scalar(idx[:, par, :], keys[:, bass.ds(n, 1), :].rearrange("p o s -> p (o s)"),
                                        -1.0, float(N), op0=ALU.mult, op1=ALU.add).then_inc(idx_ready[par], 1)
                nc.vector.tensor_scalar(pen[:, par, :], keys[:, bass.ds(n, 1), :].rearrange("p o s -> p (o s)"),
                                        0.0, NEG, op0=ALU.is_equal, op1=ALU.mult)

            def score(k, par):
                v = nc.vector
                dve.wait_ge(gathered[par], 16 * K * (k + 1))
                v.tensor_tensor(sc[:, par, :], slots[:, par, :, D], pen[:, par, :], op=ALU.add)
                v.drain()
                v.tensor_reduce(rmax[:, par, :], sc[:, par, :], axis=AX.X, op=ALU.max)
                v.drain()
                v.tensor_scalar(nmax[:, par, :], rmax[:, par, :], -1.0, -NEG / 10, op0=ALU.mult, op1=ALU.min)\
                 .then_inc(sc_ready[par], 1)

            def spread(k, par):
                v = nc.vector
                dve.wait_ge(wt_ready[par], k + 1)
                v.tensor_tensor(diag[:, par, :, :], ident[:, :].unsqueeze(1).broadcast_to([P, K, P]),
                                wt[:, par, :].unsqueeze(2).broadcast_to([P, K, P]), op=ALU.mult)\
                 .then_inc(diag_ready[par], 1)
                v.tensor_scalar(dmax[:, par, :], den[:, par, :], 1e-30, None, op0=ALU.max)
                v.drain()
                v.reciprocal(rden[:, par, :], dmax[:, par, :])
                v.drain()

            def finish(k, par):
                dve.wait_ge(acc_ready[par], ready(k))
                dve.wait_ge(xt_in[par], 16 * (k + 1))
                if not (isinstance(k, int) and k == 0):
                    dve.wait_ge(ot_out[par], 16 * k)
                nc.vector.scalar_tensor_tensor(ot[:, par, :], in0=acc[par][:, :], scalar=rden[:, par, :],
                                               in1=xt[:, par, :], op0=ALU.mult, op1=ALU.add)\
                  .then_inc(ot_ready[par], 1)

            def step(k, par, first=False, scan_too=True, last=False):
                if first:
                    issue(k, par)
                if not last:
                    issue(*after(k, par))
                if scan_too:
                    scan(k + LAG // 2, par)
                score(k, par)
                if not first:
                    finish(*before(k, par))
                spread(k, par)
                if last:
                    finish(k, par)

            steps(dve, step)

            v = nc.vector
            v.drain()
            v.tensor_tensor(lost[:, :], deg[:, :], found[:, :], op=ALU.subtract).then_inc(lost_ready, 1)
            dve.wait_ge(lost_psum, 1)
            v.tensor_scalar(tflag[:, :], pT[0][0:1, 0:T], 0.0, None, op0=ALU.is_gt, op1=ALU.add,
                            accum_out=nflag[:, :])
            v.drain()
            v.tensor_tensor(tkey[:, :], tflag[:, :], tord[:, :], op=ALU.mult)
            v.tensor_copy(ntiles[:, :], nflag[:, :])
            v.drain()
            for g in range(T // 8):
                v.max(out=tlist[:, 8 * g:8 * g + 8], in_=tkey[:, :])
                v.drain()
                v.match_replace(out=tkey[:, :], in_to_replace=tlist[:, 8 * g:8 * g + 8], in_values=tkey[:, :],
                                imm_value=0.0)
                v.drain()
            v.tensor_scalar(tiles[:, :], tlist[:, :], -1.0, float(T), op0=ALU.mult, op1=ALU.add)
            v.drain().then_inc(list_ready, 1)

            dve.wait_ge(list_ready, 1)
            count = dve.value_load(ntiles[0:1, 0:1], min_val=0, max_val=T)
            with dve.If(count > 0):
                dve.wait_ge(et_psum, 1)
                v.tensor_copy(eT[:, :], pz[0][0:T, 0:P]).then_inc(et_ready, 1)
                with dve.Fori(0, count) as r:
                    dve.wait_ge(g_adj, 16 * (r + 1))
                    v.tensor_scalar(g_mask_f, g_mask_i, 0.0, NEG, op0=ALU.is_le, op1=ALU.mult)
                    v.drain()
                    dve.wait_ge(g_e, 16 * (r + 1))
                    v.tensor_tensor(g_w_f, g_w_f, g_mask_f, op=ALU.add)
                    v.drain()
                    v.tensor_reduce(rmax[:, 0, :], g_w_f, axis=AX.X, op=ALU.max)
                    v.drain()
                    v.tensor_scalar(nmax[:, 0, :], rmax[:, 0, :], -1.0, -NEG / 10, op0=ALU.mult, op1=ALU.min)\
                     .then_inc(g_nmax, 1)
                    dve.wait_ge(g_w, r + 1)
                    v.tensor_scalar(dmax[:, 0, :], den[:, 0, :], 1e-30, None, op0=ALU.max)
                    v.drain()
                    v.reciprocal(rden[:, 0, :], dmax[:, 0, :])
                    for q in range(NQ):
                        dve.wait_ge(g_tr[q % 2], NQ // 2 * r + q // 2 + 1)
                        if q >= 2:
                            dve.wait_ge(g_mm[q % 2], NQ // 2 * r + q // 2)
                        v.tensor_copy(g_wTs[q % 2], packed[q % 2][0][:, :]).then_inc(g_wT[q % 2], 1)
                    dve.wait_ge(g_mm[1], NQ // 2 * (r + 1))
                    dve.wait_ge(g_x, 16 * (r + 1))
                    v.scalar_tensor_tensor(ot[:, 0, :], in0=acc[0][:, :], scalar=rden[:, 0, :], in1=xt[:, 0, :],
                                           op0=ALU.mult, op1=ALU.add).then_inc(g_ot, 1)


_INS = ['x', 'adj', 'L0_gnn_W', 'L0_gnn_b', 'L0_gnn_a']


def kernel(**inputs):
    import numpy as _np
    import concourse.bacc as _bacc
    from concourse import mybir as _mybir
    from concourse.bass_utils import run_bass_kernel_spmd as _run

    nc = _bacc.Bacc("TRN2", target_bir_lowering=False, num_devices=1)
    arrays, args = {}, []
    for name in _INS:
        v = _np.ascontiguousarray(inputs[name])
        arrays[f"in_{name}_dram"] = v
        args.append(nc.dram_tensor(f"in_{name}_dram", v.shape, _mybir.dt.from_np(v.dtype), kind="ExternalInput").ap())
    out = nc.dram_tensor("out_dram", args[0].shape, _mybir.dt.float32, kind="ExternalOutput").ap()
    gnn_layer(nc, *args, out)
    return _run(nc, [arrays], core_ids=[0]).results[0]["out_dram"]
```

```python
import concourse.bass as bass
from concourse import mybir
from contextlib import ExitStack


def gnn_layer(nc: bass.Bass, x: bass.AP, adj: bass.AP, W: bass.AP, b: bass.AP, a: bass.AP, out: bass.AP):
    f32, bf16, i32, u32 = mybir.dt.float32, mybir.dt.bfloat16, mybir.dt.int32, mybir.dt.uint32
    ALU, ACT, AX = mybir.AluOpType, mybir.ActivationFunctionType, mybir.AxisListType

    P = 128
    N, D = x.shape
    T = N // P
    DK = D // P
    HALF = N // 2
    NBLK = 8
    BW = N // NBLK
    BANK = 512
    NB = BW // BANK
    NCH = 4
    CW = BW // NCH
    NF = NCH * 8
    K = 16
    NG = 5
    CAP = NG * P
    LW = K + 2
    TW = D + 2
    ONE, E = D, D + 1
    NEG = -1e30
    EPS = 1e-5
    BATCH = 8
    NBATCH = T // BATCH
    NPAIR = BATCH // 2
    QUAD = 4
    LAG = NBATCH
    GB = 8
    EXPMASK, MANT, EBIAS = 0x7F800000, 23, 127

    table = nc.dram_tensor("table", (N, TW), f32, kind="Internal").ap()
    erow = nc.dram_tensor("erow", (T, P), f32, kind="Internal").ap()
    x_b = x.rearrange("(n i p) d -> n p i d", p=P, i=BATCH)
    x_t = x.rearrange("(t p) d -> t p d", p=P)
    out_t = out.rearrange("(t p) d -> t p d", p=P)
    adj_t = adj.rearrange("(t p) (h c) -> t h p c", p=P, h=2)
    table_q = table.rearrange("(q i p) c -> q p i c", p=P, i=QUAD)
    table_g = table.rearrange("(g i p) c -> g p i c", p=P, i=GB)

    with ExitStack() as ctx:
        def sb(name, shape, dt):
            return ctx.enter_context(nc.sbuf_tensor(name, shape, dt))

        def ps(name, shape, dt=f32):
            return ctx.enter_context(nc.psum_tensor(name, shape, dt))

        def sem(name):
            return ctx.enter_context(nc.semaphore(name))

        ident = sb("ident", [P, P], f32)
        shifts = sb("shifts", [P, NBLK, P], bf16)
        ones = sb("ones", [P, P], f32)
        base = sb("base", [P, NCH, 8], f32)
        w_sb = sb("w_sb", [P, DK, D], f32)
        bias = sb("bias", [P, D], f32)
        avec = sb("avec", [P, D], f32)
        adj_sb = sb("adj_sb", [P, 2, 2, HALF], i32)
        mask = sb("mask", [P, 2, 2, HALF], bf16)
        halfdeg = sb("halfdeg", [P, 2, T], f32)
        deg = sb("deg", [P, T], f32)
        found = sb("found", [P, T], f32)
        vals = sb("vals", [P, 2, NF], f32)
        pos = sb("pos", [P, NF], u32)
        expo = sb("expo", [P, 2, NF], i32)
        col = sb("col", [P, NF], f32)
        key = sb("key", [P, 2, NF], f32)
        key2 = sb("key2", [P, 2 * NF], f32)
        top = sb("top", [P, K], f32)
        junk16 = sb("junk16", [P, K], f32)
        lists = sb("lists", [P, T, LW], f32)
        upto = sb("upto", [P, P], f32)
        place = sb("place", [P, CAP], f32)
        nth = sb("nth", [P, NG, K], f32)
        number = sb("number", [P, P], f32)
        ends = sb("ends", [P, 1], f32)
        begun = sb("begun", [P, CAP], f32)
        band = sb("band", [P, 2, CAP], f32)
        which = sb("which", [P, 2, NG, K], f32)
        edge = sb("edge", [P, NG, K], f32)
        ekey = sb("ekey", [P, NG], f32)
        idx = sb("idx", [P, 2, NG], u32)
        owner = sb("owner", [P, 2, NG], f32)
        slots = sb("slots", [P, 2, NG, TW], f32)
        back = sb("back", [P, 2, NG, P], f32)
        pen = sb("pen", [P, K], f32)
        which_e = sb("which_e", [P, 2, NG, K], f32)
        sc = sb("sc", [P, K], f32)
        rmax = sb("rmax", [P, 1], f32)
        nmax = sb("nmax", [P, 1], f32)
        arg = sb("arg", [P, NG], f32)
        wt = sb("wt", [P, 2, NG], f32)
        wback = sb("wback", [P, 2, NG, P], f32)
        dmax = sb("dmax", [P, 1], f32)
        rden = sb("rden", [P, 1], f32)
        xt = sb("xt", [P, 2, D], f32)
        ot = sb("ot", [P, 2, D], f32)
        xb = sb("xb", [P, 2, GB * TW], f32)
        xrows = xb[:, :, 0:BATCH * D].rearrange("p b (i d) -> p b i d", d=D)
        stats = sb("stats", [P, BATCH, 6], f32)
        msum = sb("msum", [P, BATCH], f32)
        mdif = sb("mdif", [P, BATCH], f32)
        var = sb("var", [P, BATCH], f32)
        std = sb("std", [P, BATCH], f32)
        rstd = sb("rstd", [P, 2, BATCH], f32)
        nmr = sb("nmr", [P, 2, BATCH], f32)
        h = sb("h", [P, 2, 2, D], f32)
        hT = sb("hT", [P, 2, 2 * D], f32)
        zb = sb("zb", [P, 2, 2, D], f32)
        th = sb("th", [P, 2, 2, D], f32)
        stage = sb("stage", [P, 2, QUAD, TW], f32)
        hsum = sb("hsum", [P, 2, QUAD], f32)
        escore = sb("escore", [P, 2, QUAD], f32)
        epen = sb("epen", [P, 2, QUAD], f32)
        escores = sb("escores", [P, T], f32)
        lost = sb("lost", [P, 2, T], f32)
        tover = sb("tover", [1, T], f32)
        den = sb("den", [P, 1], f32)
        tord = sb("tord", [1, T], f32)
        tflag = sb("tflag", [1, T], f32)
        tkey = sb("tkey", [1, T], f32)
        tlist = sb("tlist", [1, T], f32)
        tiles = sb("tiles", [1, T], i32)
        nflag = sb("nflag", [1, 1], f32)
        ntiles = sb("ntiles", [1, 1], i32)
        eT = sb("eT", [T, P], f32)

        packed = [[ps(f"packed{p}{n}", [P, BANK]) for n in range(NB)] for p in range(2)]
        pT = [ps(f"pT{p}", [P, BANK]) for p in range(2)]
        pz = [ps(f"pz{p}", [P, BANK]) for p in range(2)]
        acc = pT
        found_at = pz[0][:, 0:NG * LW].rearrange("p (g w) -> p g w", w=LW)
        es = pz[1][:, 0:K]
        end = pz[0][:, NG * LW:NG * LW + 1]
        nmax_at = pz[1][:, 2 * K:2 * K + NG]

        consts = sem("consts")
        gconst = sem("gconst")
        params_in = sem("params_in")
        x_in = [sem(f"x_in{p}") for p in range(2)]
        var_ready = sem("var_ready")
        std_ready = sem("std_ready")
        rstd_ready = sem("rstd_ready")
        h_ready = [sem(f"h_ready{p}") for p in range(2)]
        hT_psum = [sem(f"hT_psum{p}") for p in range(2)]
        hT_ready = [sem(f"hT_ready{p}") for p in range(2)]
        z_psum = [sem(f"z_psum{p}") for p in range(2)]
        z_staged = [sem(f"z_staged{p}") for p in range(2)]
        zb_ready = [sem(f"zb_ready{p}") for p in range(2)]
        th_ready = [sem(f"th_ready{p}") for p in range(2)]
        dotted = [sem(f"dotted{p}") for p in range(2)]
        staged = sem("staged")
        stored = sem("stored")
        stage_free = [sem(f"stage_free{p}") for p in range(2)]
        adj_in = [[sem(f"adj_in{p}{i}") for i in range(2)] for p in range(2)]
        adj_free = [[sem(f"adj_free{p}{i}") for i in range(2)] for p in range(2)]
        mask_free = [[sem(f"mask_free{p}{i}") for i in range(2)] for p in range(2)]
        packed_free = [sem(f"packed_free{p}") for p in range(2)]
        idx_ready = sem("idx_ready")
        gathering = sem("gathering")
        gathered = [sem(f"gathered{p}") for p in range(2)]
        back_ready = sem("back_ready")
        which_e_ready = sem("which_e_ready")
        es_ready = sem("es_ready")
        nmax_ready = sem("nmax_ready")
        nmax_at_ready = sem("nmax_at_ready")
        arg_ready = sem("arg_ready")
        wt_ready = sem("wt_ready")
        wback_ready = sem("wback_ready")
        acc_ready = sem("acc_ready")
        band_ready = sem("band_ready")
        found_at_ready = sem("found_at_ready")
        end_ready = sem("end_ready")
        end_used = sem("end_used")
        xt_in = [sem(f"xt_in{p}") for p in range(2)]
        ot_ready = sem("ot_ready")
        ot_out = [sem(f"ot_out{p}") for p in range(2)]
        lost_ready = sem("lost_ready")
        lost_psum = sem("lost_psum")
        list_ready = sem("list_ready")
        et_psum = sem("et_psum")
        et_ready = sem("et_ready")
        erow_out = sem("erow_out")
        g_adj = sem("g_adj")
        g_e = sem("g_e")
        g_x = sem("g_x")
        g_table = [sem(f"g_table{p}") for p in range(2)]
        g_nmax = sem("g_nmax")
        g_w = sem("g_w")
        g_tr = [sem(f"g_tr{p}") for p in range(2)]
        g_wT = [sem(f"g_wT{p}") for p in range(2)]
        g_mm = [sem(f"g_mm{p}") for p in range(2)]
        g_acc = sem("g_acc")
        g_ot = sem("g_ot")
        g_out = sem("g_out")
        g_stored = sem("g_stored")

        g_mask_i = adj_sb[:, 0, :, :].rearrange("p h c -> p (h c)")
        g_mask_f = g_mask_i.bitcast(f32)
        g_w_f = adj_sb[:, 1, :, :].rearrange("p h c -> p (h c)").bitcast(f32)
        g_tab = [xb[:, p, 0:GB * TW].rearrange("p (i c) -> p i c", c=TW) for p in range(2)]
        g_wTs = [wback[:, p, 0:4, :].rearrange("p k c -> p (k c)") for p in range(2)]
        NL = T // GB
        NQ = T // 4

        NCONST = 10 + NBLK

        block = ctx.enter_context(nc.Block())

        def steps(engine, step, scans):
            full = scans // 2
            for k in range(2):
                for par in range(2):
                    step(k, par, first=(k + par == 0))
            with engine.Fori(2, full) as k:
                step(k, 0)
                step(k, 1)
            if scans % 2:
                step(full, 0)
                step(full, 1, scanning=False)
                full += 1
            with engine.Fori(full, T // 2 - 2) as k:
                step(k, 0, scanning=False)
                step(k, 1, scanning=False)
            step(T // 2 - 2, 0, scanning=False)
            step(T // 2 - 2, 1, scanning=False, ahead=2)
            step(T // 2 - 1, 0, scanning=False, ahead=1)
            step(T // 2 - 1, 1, scanning=False, ahead=0)

        def free(m):
            return m + 1

        def ready(m):
            return m + 2

        def free2(n):
            return n + 1

        def ready2(n):
            return n + 3

        def after(k, par):
            return (k, 1) if par == 0 else (k + 1, 0)

        def use(d, bp, j):
            return NPAIR // 2 * (2 * d + bp) + j // 2, j % 2

        def next_batch(d, bp):
            return (d, 1) if bp == 0 else (d + 1, 0)

        def pair(d, bp, j):
            if j >= NPAIR:
                d, bp = next_batch(d, bp)
                j -= NPAIR
            return None if isinstance(d, int) and d == NBATCH // 2 else (d, bp, j)

        def before(k, par):
            return (k, 0) if par == 1 else (k - 1, 1)

        @block.sync
        def _(sp):
            sp.dma_start(w_sb[:, :, :], W.rearrange("(k p) d -> p k d", p=P)).then_inc(params_in, 16)
            sp.dma_start(bias[:, :], b.partition_broadcast(P)).then_inc(params_in, 16)
            sp.dma_start(avec[:, :], a.rearrange("d o -> (o d)").partition_broadcast(P)).then_inc(params_in, 16)
            with sp.Fori(0, T // 2) as k:
                for par in range(2):
                    for i in range(2):
                        sp.wait_ge(adj_free[par][i], free(k))
                        sp.dma_start(adj_sb[:, par, i, :],
                                     adj_t[bass.ds(2 * k + par, 1), i, :, :].rearrange("o p c -> (o p) c"))\
                          .then_inc(adj_in[par][i], 16)

            sp.wait_ge(list_ready, 1)
            count = sp.value_load(ntiles[0:1, 0:1], min_val=0, max_val=T)
            with sp.If(count > 0):
                for par in range(2):
                    sp.wait_ge(ot_out[par], 16 * (T // 2))
                sp.wait_ge(et_ready, 1)
                sp.dma_start(erow[:, :], eT[:, :]).then_inc(erow_out, 16)
                sp.wait_ge(erow_out, 16)
                sp.sem_inc(g_stored, 1)
                with sp.Fori(0, count) as r:
                    tile = sp.value_load(tiles[0:1, bass.ds(r, 1)], min_val=0, max_val=T - 1)
                    sp.wait_ge(g_stored, free(r))
                    sp.dma_start(g_mask_i, adj[bass.ds(tile * P, P), :]).then_inc(g_adj, 16)
                    sp.dma_start(g_w_f, erow.rearrange("t p -> (t p)").partition_broadcast(P)).then_inc(g_e, 16)
                    sp.dma_start(xt[:, 0, :], x[bass.ds(tile * P, P), :]).then_inc(g_x, 16)
                    for g in range(NL):
                        if g >= 2:
                            sp.wait_ge(g_mm[1], NQ // 2 * r + g - 1)
                        sp.dma_start(g_tab[g % 2], table_g[g]).then_inc(g_table[g % 2], 16)
                    sp.wait_ge(g_ot, r + 1)
                    sp.dma_start(out[bass.ds(tile * P, P), :], ot[:, 0, :]).then_inc(g_out, 16)
                    sp.wait_ge(g_out, 16 * (r + 1))
                    sp.sem_inc(g_stored, 1)

        @block.gpsimd
        def _(pool):
            for q in range(2):
                pool.sem_inc(stage_free[q], 1)
            nc.gpsimd.memset(ident[:, :], 0.0).then_inc(gconst, 1)
            nc.gpsimd.memset(shifts[:, :, :], 0.0).then_inc(gconst, 1)
            nc.gpsimd.memset(ones[:, :], 1.0).then_inc(gconst, 1)
            nc.gpsimd.memset(stage[:, :, :, ONE], 1.0).then_inc(consts, 1)
            nc.gpsimd.memset(slots[:, :, :, :], 0.0).then_inc(consts, 1)
            nc.gpsimd.iota(lists[:, :, K + 1], pattern=[[0, T]], base=1, channel_multiplier=1,
                           allow_small_or_imprecise_dtypes=True).then_inc(consts, 1)
            nc.gpsimd.iota(place[:, :], pattern=[[1, CAP]], base=0, channel_multiplier=0,
                           allow_small_or_imprecise_dtypes=True).then_inc(consts, 1)
            nc.gpsimd.iota(nth[:, :, :], pattern=[[P, NG], [-1, K]], base=0, channel_multiplier=1,
                           allow_small_or_imprecise_dtypes=True).then_inc(consts, 1)
            nc.gpsimd.iota(number[:, :], pattern=[[1, P]], base=1, channel_multiplier=0,
                           allow_small_or_imprecise_dtypes=True).then_inc(consts, 1)
            nc.gpsimd.iota(base[:, :, :], pattern=[[-CW, NCH], [0, 8]], base=N + EBIAS * BW,
                           channel_multiplier=0, allow_small_or_imprecise_dtypes=True).then_inc(consts, 1)
            nc.gpsimd.iota(tord[:, :], pattern=[[-1, T]], base=T, channel_multiplier=0,
                           allow_small_or_imprecise_dtypes=True).then_inc(consts, 1)
            pool.wait_ge(gconst, 3)
            nc.gpsimd.affine_select(out=ident[:, :], in_=ident[:, :], compare_op=ALU.not_equal, fill=1.0,
                                    base=0, pattern=[[-1, P]], channel_multiplier=1).then_inc(consts, 1)
            nc.gpsimd.affine_select(out=upto[:, :], in_=ones[:, :], compare_op=ALU.is_ge, fill=0.0,
                                    base=0, pattern=[[1, P]], channel_multiplier=-1).then_inc(consts, 1)
            for j in range(NBLK):
                nc.gpsimd.affine_select(out=shifts[:, j, :], in_=shifts[:, j, :], compare_op=ALU.not_equal,
                                        fill=float(2 ** j), base=0, pattern=[[-1, P]],
                                        channel_multiplier=1).then_inc(consts, 1)
            for n in range(NBATCH):
                for q in range(BATCH // QUAD):
                    g = n * (BATCH // QUAD) + q
                    pool.wait_ge(staged, g + 1)
                    pool.dma_start(table_q[g], stage[:, g % 2, :, :]).then_inc(stored, 16)
                    pool.wait_ge(stored, 16 * (g + 1))
                    pool.sem_inc(stage_free[g % 2], 1)

            last_row = pool.alloc_register("last_row")
            pool.reg_mov(last_row, N - 1)

            def gather(k, par):
                n = 2 * k + par
                pool.wait_ge(idx_ready, n + 1)
                pool.wait_ge(acc_ready, free2(n))
                pool.sem_inc(gathering, 1)
                for g in range(NG):
                    pool.indirect_dma_start(
                        out=slots[:, par, g, :], out_offset=None, in_=table[:, :],
                        in_offset=bass.IndirectOffsetOnAxis(ap=idx[:, par, g:g + 1], axis=0),
                        bounds_check=last_row, oob_is_err=False).then_inc(gathered[par], 16)
                for g in range(NG):
                    last = nc.gpsimd.tensor_scalar(back[:, par, g, :], number[:, :], owner[:, par, g:g + 1], None,
                                                   op0=ALU.is_equal)
                last.then_inc(back_ready, 1)

            with pool.Fori(0, T // 2) as k:
                gather(k, 0)
                gather(k, 1)

        @block.scalar
        def _(act):
            for par in range(2):
                act.dma_start(xrows[:, par, :, :], x_b[par]).then_inc(x_in[par], 16)
            for par in range(2):
                for i in range(2):
                    act.sem_inc(adj_free[par][i], 1)

            def scan(k, par, halves=(0, 1)):
                for i in halves:
                    act.wait_ge(adj_in[par][i], 16 * (k + 1))
                    act.wait_ge(mask_free[par][i], free(k))
                    nc.scalar.activation(mask[:, par, i, :], adj_sb[:, par, i, :], ACT.Relu,
                                         accum_out=halfdeg[:, i, bass.ds(2 * k + par, 1)])\
                      .then_inc(adj_free[par][i], 1)

            def relu(d, bp, j):
                m, u = use(d, bp, j)
                act.wait_ge(hT_psum[u], free(m))
                for i in range(2):
                    t = 2 * j + i
                    last = nc.scalar.activation(h[:, u, i, :], xrows[:, bp, t, :], ACT.Relu,
                                                scale=rstd[:, bp, t:t + 1], bias=nmr[:, bp, t:t + 1])
                last.then_inc(h_ready[u], 1)

            def load_batch(d, bp):
                for u in range(2):
                    act.wait_ge(h_ready[u], ready(use(d, bp, NPAIR - 2)[0]))
                act.dma_start(xrows[:, bp, :, :], x_b[bass.ds(2 * d + 2 + bp, 1)].rearrange("o p i d -> (o p) i d"))\
                   .then_inc(x_in[bp], 16)

            def stage_z(d, bp, j):
                m, u = use(d, bp, j)
                q, i = j // 2, 2 * (j % 2)
                act.wait_ge(z_psum[u], ready(m))
                if i == 0:
                    act.wait_ge(stage_free[q], free(2 * d + bp))
                nc.scalar.copy(stage[:, q, i:i + 2, 0:D], pz[u].rearrange("p (i d) -> p i d", d=D))\
                  .then_inc(z_staged[u], 1)

            def tanh(d, bp, j):
                m, u = use(d, bp, j)
                act.wait_ge(zb_ready[u], ready(m))
                act.wait_ge(dotted[u], free(m))
                for i in range(2):
                    t = 2 * (j % 2) + i
                    last = nc.scalar.activation(th[:, u, i, :], zb[:, u, i, :], ACT.Tanh,
                                                accum_out=hsum[:, j // 2, t:t + 1])
                last.then_inc(th_ready[u], 1)

            def root(d, bp):
                act.wait_ge(var_ready, 2 * d + bp + 1)
                nc.scalar.activation(std[:, :], var[:, :], ACT.Sqrt).then_inc(std_ready, 1)

            def project(d):
                for bp in range(2):
                    for j in range(NPAIR):
                        stage_z(d, bp, j)
                        ahead = pair(d, bp, j + 2)
                        if ahead:
                            if ahead[2] == 0:
                                act.wait_ge(rstd_ready, 2 * ahead[0] + ahead[1] + 1)
                            relu(*ahead)
                        tanh(d, bp, j)
                        if j == 1:
                            if not isinstance(d, int):
                                load_batch(d, bp)
                            if ahead and pair(d, bp, NPAIR):
                                root(*next_batch(d, bp))
                        if j < 2:
                            scan(d, bp, [j])

            for u in range(2):
                act.sem_inc(h_ready[u], 1)
                act.sem_inc(z_staged[u], 1)
                act.sem_inc(th_ready[u], 1)
            root(0, 0)
            act.wait_ge(rstd_ready, 1)
            relu(0, 0, 0)
            relu(0, 0, 1)
            with act.Fori(0, NBATCH // 2 - 1) as d:
                project(d)
            project(NBATCH // 2 - 1)

            def load_x(k, par):
                act.wait_ge(ot_ready, free2(2 * k + par))
                act.dma_start(xt[:, par, :], x_t[bass.ds(2 * k + par, 1), :, :].rearrange("o p d -> (o p) d"))\
                   .then_inc(xt_in[par], 16)

            def store(k, par):
                act.wait_ge(ot_ready, ready2(2 * k + par))
                act.dma_start(out_t[bass.ds(2 * k + par, 1), :, :].rearrange("o p d -> (o p) d"), ot[:, par, :])\
                   .then_inc(ot_out[par], 16)

            def step(k, par, first=False, scanning=True, ahead=3):
                if scanning:
                    scan(k + LAG // 2 + 1, par, [0])
                act.wait_ge(arg_ready, 2 * k + par + 1)
                nc.scalar.activation(wt[:, par, :], arg[:, :], ACT.Exp).then_inc(wt_ready, 1)
                if scanning:
                    scan(k + LAG // 2 + 1, par, [1])
                if not first:
                    store(*before(k, par))
                load_x(k, par)

            scan(LAG // 2, 0)
            scan(LAG // 2, 1)
            steps(act, step, T - LAG - 2)
            store(T // 2 - 1, 1)
            for par in range(2):
                act.wait_ge(ot_out[par], 16 * (T // 2))

            act.wait_ge(list_ready, 1)
            count = act.value_load(ntiles[0:1, 0:1], min_val=0, max_val=T)
            with act.If(count > 0):
                with act.Fori(0, count) as r:
                    act.wait_ge(g_nmax, r + 1)
                    nc.scalar.activation(g_w_f, g_w_f, ACT.Exp, bias=nmax[:, :],
                                         accum_out=den[:, :]).then_inc(g_w, 1)

        @block.tensor
        def _(pe):
            for par in range(2):
                pe.sem_inc(hT_psum[par], 1)
                pe.sem_inc(z_psum[par], 1)
                pe.sem_inc(acc_ready, 1)
                for i in range(2):
                    pe.sem_inc(mask_free[par][i], 1)
            pe.wait_ge(consts, NCONST)
            pe.wait_ge(params_in, 48)

            def pack(k, par, halves=(0, 1)):
                for i in halves:
                    pe.wait_ge(adj_free[par][i], ready(k))
                    if i == 0:
                        pe.wait_ge(packed_free[par], free(k))
                    for j in range(NBLK // 2):
                        for n in range(NB):
                            last = nc.tensor.matmul(packed[par][n][:, :], shifts[:, i * NBLK // 2 + j, :],
                                                    mask[:, par, i, j * BW + n * BANK:j * BW + (n + 1) * BANK],
                                                    start=(i == 0 and j == 0), stop=(i == 1 and j == NBLK // 2 - 1))
                    last.then_inc(mask_free[par][i], 1)

            def turn(d, bp, j):
                m, u = use(d, bp, j)
                pe.wait_ge(h_ready[u], ready(m))
                pe.wait_ge(hT_ready[u], free(m))
                for i in range(2):
                    for c in range(DK):
                        last = nc.tensor.transpose(pT[u][:, i * D + c * P:i * D + (c + 1) * P],
                                                   h[:, u, i, c * P:(c + 1) * P], ident[:, :])
                last.then_inc(hT_psum[u], 1)

            def multiply(d, bp, j):
                m, u = use(d, bp, j)
                pe.wait_ge(hT_ready[u], ready(m))
                pe.wait_ge(z_staged[u], free(m))
                for i in range(2):
                    for c in range(DK):
                        last = nc.tensor.matmul(pz[u][:, i * D:(i + 1) * D],
                                                hT[:, u, i * D + c * P:i * D + (c + 1) * P], w_sb[:, c, :],
                                                start=(c == 0), stop=(c == DK - 1))
                last.then_inc(z_psum[u], 1)

            def project(d):
                for bp in range(2):
                    for j in range(NPAIR):
                        if pair(d, bp, j + 1):
                            multiply(*pair(d, bp, j + 1))
                        if pair(d, bp, j + 2):
                            turn(*pair(d, bp, j + 2))
                        if 1 <= j < 3:
                            pack(d, bp, [j - 1])

            turn(0, 0, 0)
            multiply(0, 0, 0)
            turn(0, 0, 1)
            with pe.Fori(0, NBATCH // 2 - 1) as d:
                project(d)
            project(NBATCH // 2 - 1)
            for u in range(2):
                pe.wait_ge(z_staged[u], ready(T // 4 - 1))

            def prefix(n):
                nc.tensor.matmul(end, upto[:, :], found[:, bass.ds(n, 1)], start=True, stop=True).then_inc(end_ready, 1)

            def look_up(k, par, ahead=True):
                n = 2 * k + par
                pe.wait_ge(band_ready, n + 1)
                if ahead:
                    prefix(n + 1)
                for g in range(NG):
                    last = nc.tensor.matmul(found_at[:, g, :], band[:, par, g * P:(g + 1) * P],
                                            lists[:, bass.ds(n, 1), :].rearrange("p o w -> p (o w)"),
                                            start=True, stop=True)
                last.then_inc(found_at_ready, 1)

            def scores_back(k, par):
                n = 2 * k + par
                pe.wait_ge(back_ready, n + 1)
                pe.wait_ge(which_e_ready, n + 1)
                for g in range(NG):
                    last = nc.tensor.matmul(es, back[:, par, g, :], which_e[:, par, g, :],
                                            start=(g == 0), stop=(g == NG - 1))
                last.then_inc(es_ready, 1)

            def max_out(k, par):
                pe.wait_ge(nmax_ready, 2 * k + par + 1)
                for g in range(NG):
                    last = nc.tensor.matmul(nmax_at[:, g:g + 1], band[:, par, g * P:(g + 1) * P], nmax[:, :],
                                            start=True, stop=True)
                last.then_inc(nmax_at_ready, 1)

            def sum_edges(k, par):
                n = 2 * k + par
                pe.wait_ge(wback_ready, n + 1)
                pe.wait_ge(ot_ready, free2(n))
                for g in range(NG):
                    last = nc.tensor.matmul(acc[par][:, 0:D + 1], wback[:, par, g, :], slots[:, par, g, 0:D + 1],
                                            start=(g == 0), stop=(g == NG - 1))
                last.then_inc(acc_ready, 1)

            def step(k, par, first=False, scanning=True, ahead=3):
                scores_back(k, par)
                max_out(k, par)
                if ahead >= 2:
                    look_up(k + 1, par, ahead=(ahead == 3))
                if scanning:
                    pack(*after(k + LAG // 2, par))
                sum_edges(k, par)

            pack(LAG // 2, 0)
            prefix(0)
            for par in range(2):
                look_up(0, par)
            steps(pe, step, T - LAG - 1)

            pe.wait_ge(lost_ready, 1)
            nc.tensor.matmul(pT[0][:, 0:2 * T], ones[:, :], lost[:, :, :].rearrange("p a t -> p (a t)"),
                             start=True, stop=True).then_inc(lost_psum, 1)

            pe.wait_ge(list_ready, 1)
            count = pe.value_load(ntiles[0:1, 0:1], min_val=0, max_val=T)
            with pe.If(count > 0):
                nc.tensor.transpose(pz[0][0:T, 0:P], escores[:, :], ident[:, :]).then_inc(et_psum, 1)
                with pe.Fori(0, count) as r:
                    def products(q):
                        pe.wait_ge(g_wT[q % 2], NQ // 2 * r + q // 2 + 1)
                        g = q // 2
                        pe.wait_ge(g_table[g % 2], 16 * (NL // 2 * r + g // 2 + 1))
                        for c in range(4):
                            last = nc.tensor.matmul(acc[0][:, 0:D], g_wTs[q % 2][:, c * P:(c + 1) * P],
                                                    g_tab[g % 2][:, 4 * (q % 2) + c, 0:D],
                                                    start=(q == 0 and c == 0), stop=(q == NQ - 1 and c == 3))
                        last.then_inc(g_mm[q % 2], 1)
                        return last

                    pe.wait_ge(g_w, r + 1)
                    for q in range(NQ):
                        if q >= 2:
                            pe.wait_ge(g_wT[q % 2], NQ // 2 * r + q // 2)
                        for c in range(4):
                            last = nc.tensor.transpose(packed[q % 2][0][:, c * P:(c + 1) * P],
                                                       g_w_f[:, (4 * q + c) * P:(4 * q + c + 1) * P], ident[:, :])
                        last.then_inc(g_tr[q % 2], 1)
                        if q >= 1:
                            products(q - 1)
                    products(NQ - 1)

        @block.vector
        def _(dve):
            for par in range(2):
                dve.sem_inc(packed_free[par], 1)
                dve.sem_inc(hT_ready[par], 1)
                dve.sem_inc(zb_ready[par], 1)
                dve.sem_inc(dotted[par], 1)
                dve.sem_inc(ot_ready, 1)
            dve.wait_ge(consts, NCONST)
            dve.wait_ge(params_in, 48)

            v = nc.vector

            def find(k, par):
                dve.wait_ge(mask_free[par][1], ready(k))
                v.tensor_tensor(deg[:, bass.ds(2 * k + par, 1)], halfdeg[:, 0, bass.ds(2 * k + par, 1)],
                                halfdeg[:, 1, bass.ds(2 * k + par, 1)], op=ALU.add)
                chunks = [packed[par][c * CW // BANK][:, c * CW % BANK:c * CW % BANK + CW] for c in range(NCH)]
                for c in range(NCH):
                    v.max(out=vals[:, 0, 8 * c:8 * c + 8], in_=chunks[c])
                v.drain()
                for c in range(NCH):
                    last = v.max_index(out=pos[:, 8 * c:8 * c + 8], in_max=vals[:, 0, 8 * c:8 * c + 8],
                                       in_values=chunks[c])
                last.then_inc(packed_free[par], 1)

            def collect(k, par):
                v.drain()
                v.tensor_single_scalar(expo[:, 0, :], vals[:, 0, :].bitcast(i32), EXPMASK, op=ALU.bitwise_and)
                v.drain()
                v.tensor_tensor(vals[:, 1, :], vals[:, 0, :], expo[:, 0, :].bitcast(f32), op=ALU.subtract)
                v.tensor_tensor(col[:, :], base[:, :, :].rearrange("p c e -> p (c e)"), pos[:, :], op=ALU.subtract)
                v.drain()
                v.tensor_single_scalar(expo[:, :, :], vals[:, :, :].bitcast(i32), MANT, op=ALU.logical_shift_right)
                v.drain()
                for o in range(2):
                    v.scalar_tensor_tensor(key[:, o, :], in0=expo[:, o, :], scalar=-float(BW), in1=col[:, :],
                                           op0=ALU.mult, op1=ALU.add)
                v.drain()
                v.scalar_tensor_tensor(key2[:, :], in0=vals[:, :, :].rearrange("p o f -> p (o f)"), scalar=0.0,
                                       in1=key[:, :, :].rearrange("p o f -> p (o f)"), op0=ALU.is_gt, op1=ALU.mult)
                v.drain()
                v.max(out=top[:, 0:8], in_=key2[:, :])
                v.drain()
                v.match_replace(out=key2[:, :], in_to_replace=top[:, 0:8], in_values=key2[:, :], imm_value=0.0)
                v.drain()
                v.max(out=top[:, 8:16], in_=key2[:, :])
                v.drain()
                v.tensor_scalar(junk16[:, :], top[:, :], 0.0, None, op0=ALU.is_gt, op1=ALU.add,
                                accum_out=found[:, bass.ds(2 * k + par, 1)])
                v.tensor_scalar(lists[:, bass.ds(2 * k + par, 1), 0:K].rearrange("p o s -> p (o s)"), top[:, :],
                                1.0, None, op0=ALU.mult)
                v.drain()

            def statistics(d, bp, tiles):
                for i in tiles:
                    if i == 0:
                        dve.wait_ge(x_in[bp], 16 * (d + 1))
                    v.bn_stats(out=stats[:, i, :], in_=xrows[:, bp, i, :])

            def variance():
                v.drain()
                v.tensor_tensor(msum[:, :], stats[:, :, 1], stats[:, :, 4], op=ALU.add)
                v.tensor_tensor(mdif[:, :], stats[:, :, 1], stats[:, :, 4], op=ALU.subtract)
                v.tensor_tensor(var[:, :], stats[:, :, 2], stats[:, :, 5], op=ALU.add)
                v.drain()
                v.scalar_tensor_tensor(mdif[:, :], in0=mdif[:, :], scalar=0.25, in1=mdif[:, :],
                                       op0=ALU.mult, op1=ALU.mult)
                v.tensor_scalar(var[:, :], var[:, :], 1.0 / D, EPS, op0=ALU.mult, op1=ALU.add)
                v.drain()
                v.tensor_tensor(var[:, :], var[:, :], mdif[:, :], op=ALU.add).then_inc(var_ready, 1)

            def normaliser(d, bp):
                dve.wait_ge(std_ready, 2 * d + bp + 1)
                v.reciprocal(rstd[:, bp, :], std[:, :])
                v.drain()
                v.scalar_tensor_tensor(nmr[:, bp, :], in0=msum[:, :], scalar=-0.5, in1=rstd[:, bp, :],
                                       op0=ALU.mult, op1=ALU.mult).then_inc(rstd_ready, 1)

            def copy_hT(d, bp, j):
                m, u = use(d, bp, j)
                dve.wait_ge(hT_psum[u], ready(m))
                dve.wait_ge(z_psum[u], free(m))
                v.tensor_copy(hT[:, u, :], pT[u][:, :]).then_inc(hT_ready[u], 1)

            def add_bias(d, bp, j):
                m, u = use(d, bp, j)
                q, i = j // 2, 2 * (j % 2)
                dve.wait_ge(z_staged[u], ready(m))
                dve.wait_ge(th_ready[u], free(m))
                v.tensor_tensor(zb[:, u, :, :], stage[:, q, i:i + 2, 0:D],
                                bias[:, :].unsqueeze(1).broadcast_to([P, 2, D]), op=ALU.add)\
                 .then_inc(zb_ready[u], 1)

            def dot_a(d, bp, j):
                m, u = use(d, bp, j)
                dve.wait_ge(th_ready[u], ready(m))
                for i in range(2):
                    t = 2 * (j % 2) + i
                    last = v.scalar_tensor_tensor(th[:, u, i, :], in0=th[:, u, i, :], scalar=1.0, in1=avec[:, :],
                                                  op0=ALU.mult, op1=ALU.mult,
                                                  accum_out=escore[:, j // 2, t:t + 1])
                last.then_inc(dotted[u], 1)

            def scores(d, bp, q):
                g = 2 * (2 * d + bp) + q
                v.drain()
                v.tensor_scalar(epen[:, q, :], hsum[:, q, :], 0.0, NEG, op0=ALU.is_equal, op1=ALU.mult)
                v.drain()
                v.tensor_tensor(escores[:, bass.ds(QUAD * g, QUAD)], escore[:, q, :], epen[:, q, :], op=ALU.add)
                v.tensor_tensor(stage[:, q, :, E], escore[:, q, :], epen[:, q, :], op=ALU.add).then_inc(staged, 1)

            def project(d):
                for bp in range(2):
                    for j in range(NPAIR):
                        if pair(d, bp, j + 1):
                            copy_hT(*pair(d, bp, j + 1))
                        add_bias(d, bp, j)
                        if pair(d, bp, NPAIR):
                            if j < 2:
                                statistics(*next_batch(d, bp), range(4 * j, 4 * j + 4))
                            if j == 1:
                                variance()
                            if j == 2:
                                normaliser(*next_batch(d, bp))
                        dot_a(d, bp, j)
                        if j % 2 == 1:
                            scores(d, bp, j // 2)
                    find(d, bp)
                    collect(d, bp)

            statistics(0, 0, range(BATCH))
            variance()
            normaliser(0, 0)
            copy_hT(0, 0, 0)
            with dve.Fori(0, NBATCH // 2 - 1) as d:
                project(d)
            project(NBATCH // 2 - 1)

            def select(k, par):
                dve.wait_ge(found_at_ready, 2 * k + par + 1)
                v.tensor_tensor(which[:, par, :, :], nth[:, :, :],
                                found_at[:, :, K:K + 1].broadcast_to([P, NG, K]), op=ALU.is_equal)
                v.tensor_copy(owner[:, par, :], found_at[:, :, K + 1])
                v.drain()
                v.tensor_tensor(edge[:, :, :], which[:, par, :, :], found_at[:, :, 0:K], op=ALU.mult)
                v.drain()
                v.tensor_reduce(ekey[:, :], edge[:, :, :], axis=AX.X, op=ALU.add)
                v.drain()
                v.tensor_scalar(idx[:, par, :], ekey[:, :], -1.0, float(N), op0=ALU.mult, op1=ALU.add)\
                 .then_inc(idx_ready, 1)

            def score_edges(k, par):
                n = 2 * k + par
                dve.wait_ge(gathered[par], 16 * NG * (k + 1))
                v.tensor_tensor(which_e[:, par, :, :], which[:, par, :, :],
                                slots[:, par, :, E:E + 1].broadcast_to([P, NG, K]), op=ALU.mult)\
                 .then_inc(which_e_ready, 1)
                v.tensor_scalar(pen[:, :], lists[:, bass.ds(n, 1), 0:K].rearrange("p o s -> p (o s)"),
                                0.0, NEG, op0=ALU.is_equal, op1=ALU.mult)
                v.drain()

            def bounds(k, par):
                n = 2 * k + par
                dve.wait_ge(end_ready, n + 1)
                v.tensor_tensor(lists[:, bass.ds(n, 1), K], end, found[:, bass.ds(n, 1)], op=ALU.subtract)
                v.tensor_copy(ends[:, :], end)

            def row_max(k, par):
                dve.wait_ge(es_ready, 2 * k + par + 1)
                v.tensor_tensor(sc[:, :], es, pen[:, :], op=ALU.add)
                v.drain()
                v.tensor_reduce(rmax[:, :], sc[:, :], axis=AX.X, op=ALU.max)
                v.drain()
                v.tensor_scalar(nmax[:, :], rmax[:, :], -1.0, -NEG / 10, op0=ALU.mult, op1=ALU.min)\
                 .then_inc(nmax_ready, 1)

            def less_max(k, par):
                dve.wait_ge(nmax_at_ready, 2 * k + par + 1)
                v.tensor_tensor(arg[:, :], slots[:, par, :, E], nmax_at, op=ALU.add)
                v.drain()
                v.tensor_scalar(arg[:, :], arg[:, :], 1.0, None, op0=ALU.min).then_inc(arg_ready, 1)

            def begin(k, par):
                n = 2 * k + par
                v.drain()
                v.tensor_scalar(begun[:, :], place[:, :], lists[:, bass.ds(n, 1), K], None, op0=ALU.is_ge)
                v.drain()

            def lay_out(k, par):
                v.scalar_tensor_tensor(band[:, par, :], in0=place[:, :], scalar=ends[:, :], in1=begun[:, :],
                                       op0=ALU.is_lt, op1=ALU.mult).then_inc(band_ready, 1)

            def weigh(k, par):
                dve.wait_ge(wt_ready, 2 * k + par + 1)
                v.tensor_tensor(wback[:, par, :, :], back[:, par, :, :],
                                wt[:, par, :].unsqueeze(2).broadcast_to([P, NG, P]), op=ALU.mult)\
                 .then_inc(wback_ready, 1)

            def finish(k, par):
                n = 2 * k + par
                dve.wait_ge(acc_ready, ready2(n))
                v.tensor_scalar(dmax[:, :], acc[par][:, D:D + 1], 1e-30, None, op0=ALU.max)
                v.drain()
                v.reciprocal(rden[:, :], dmax[:, :])
                v.drain()
                dve.wait_ge(xt_in[par], 16 * (k + 1))
                if not (isinstance(k, int) and k == 0):
                    dve.wait_ge(ot_out[par], 16 * k)
                v.scalar_tensor_tensor(ot[:, par, :], in0=acc[par][:, 0:D], scalar=rden[:, :],
                                       in1=xt[:, par, :], op0=ALU.mult, op1=ALU.add).then_inc(ot_ready, 1)

            def step(k, par, first=False, scanning=True, ahead=3):
                if ahead >= 1:
                    select(*after(k, par))
                score_edges(k, par)
                if not first:
                    finish(*before(k, par))
                row_max(k, par)
                if ahead >= 2:
                    bounds(k + 1, par)
                    begin(k + 1, par)
                less_max(k, par)
                if ahead >= 2:
                    lay_out(k + 1, par)
                if scanning:
                    find(k + LAG // 2, par)
                weigh(k, par)
                if scanning:
                    collect(k + LAG // 2, par)

            for par in range(2):
                bounds(0, par)
                begin(0, par)
                lay_out(0, par)
                if par == 0:
                    select(0, 0)
            steps(dve, step, T - LAG)
            finish(T // 2 - 1, 1)

            v.drain()
            v.tensor_copy(lost[:, 1, :], found[:, :])
            v.tensor_tensor(lost[:, 0, :], deg[:, :], found[:, :], op=ALU.subtract).then_inc(lost_ready, 1)
            dve.wait_ge(lost_psum, 1)
            v.tensor_scalar(tover[:, :], pT[0][0:1, T:2 * T], float(CAP), None, op0=ALU.is_gt)
            v.drain()
            v.scalar_tensor_tensor(tflag[:, :], in0=pT[0][0:1, 0:T], scalar=0.0, in1=tover[:, :],
                                   op0=ALU.is_gt, op1=ALU.max)
            v.drain()
            v.tensor_reduce(nflag[:, :], tflag[:, :], axis=AX.X, op=ALU.add)
            v.drain()
            v.tensor_tensor(tkey[:, :], tflag[:, :], tord[:, :], op=ALU.mult)
            v.tensor_copy(ntiles[:, :], nflag[:, :])
            v.drain()
            for g in range(T // 8):
                v.max(out=tlist[:, 8 * g:8 * g + 8], in_=tkey[:, :])
                v.drain()
                v.match_replace(out=tkey[:, :], in_to_replace=tlist[:, 8 * g:8 * g + 8], in_values=tkey[:, :],
                                imm_value=0.0)
                v.drain()
            v.tensor_scalar(tiles[:, :], tlist[:, :], -1.0, float(T), op0=ALU.mult, op1=ALU.add)
            v.drain().then_inc(list_ready, 1)

            dve.wait_ge(list_ready, 1)
            count = dve.value_load(ntiles[0:1, 0:1], min_val=0, max_val=T)
            with dve.If(count > 0):
                dve.wait_ge(et_psum, 1)
                v.tensor_copy(eT[:, :], pz[0][0:T, 0:P]).then_inc(et_ready, 1)
                with dve.Fori(0, count) as r:
                    dve.wait_ge(g_adj, 16 * (r + 1))
                    v.tensor_scalar(g_mask_f, g_mask_i, 0.0, NEG, op0=ALU.is_le, op1=ALU.mult)
                    v.drain()
                    dve.wait_ge(g_e, 16 * (r + 1))
                    v.tensor_tensor(g_w_f, g_w_f, g_mask_f, op=ALU.add)
                    v.drain()
                    v.tensor_reduce(rmax[:, :], g_w_f, axis=AX.X, op=ALU.max)
                    v.drain()
                    v.tensor_scalar(nmax[:, :], rmax[:, :], -1.0, -NEG / 10, op0=ALU.mult, op1=ALU.min)\
                     .then_inc(g_nmax, 1)
                    dve.wait_ge(g_w, r + 1)
                    v.tensor_scalar(dmax[:, :], den[:, :], 1e-30, None, op0=ALU.max)
                    v.drain()
                    v.reciprocal(rden[:, :], dmax[:, :])
                    for q in range(NQ):
                        dve.wait_ge(g_tr[q % 2], NQ // 2 * r + q // 2 + 1)
                        if q >= 2:
                            dve.wait_ge(g_mm[q % 2], NQ // 2 * r + q // 2)
                        v.tensor_copy(g_wTs[q % 2], packed[q % 2][0][:, :]).then_inc(g_wT[q % 2], 1)
                    dve.wait_ge(g_mm[1], NQ // 2 * (r + 1))
                    dve.wait_ge(g_x, 16 * (r + 1))
                    v.scalar_tensor_tensor(ot[:, 0, :], in0=acc[0][:, 0:D], scalar=rden[:, :], in1=xt[:, 0, :],
                                           op0=ALU.mult, op1=ALU.add).then_inc(g_ot, 1)


_INS = ['x', 'adj', 'L0_gnn_W', 'L0_gnn_b', 'L0_gnn_a']


def kernel(**inputs):
    import numpy as _np
    import concourse.bacc as _bacc
    from concourse import mybir as _mybir
    from concourse.bass_utils import run_bass_kernel_spmd as _run

    nc = _bacc.Bacc("TRN2", target_bir_lowering=False, num_devices=1)
    arrays, args = {}, []
    for name in _INS:
        v = _np.ascontiguousarray(inputs[name])
        arrays[f"in_{name}_dram"] = v
        args.append(nc.dram_tensor(f"in_{name}_dram", v.shape, _mybir.dt.from_np(v.dtype), kind="ExternalInput").ap())
    out = nc.dram_tensor("out_dram", args[0].shape, _mybir.dt.float32, kind="ExternalOutput").ap()
    gnn_layer(nc, *args, out)
    return _run(nc, [arrays], core_ids=[0]).results[0]["out_dram"]
```

```python
import concourse.bass as bass
from concourse import mybir
from contextlib import ExitStack


def gnn_layer(nc: bass.Bass, x: bass.AP, adj: bass.AP, W: bass.AP, b: bass.AP, a: bass.AP, out: bass.AP):
    f32, bf16, i32, u32 = mybir.dt.float32, mybir.dt.bfloat16, mybir.dt.int32, mybir.dt.uint32
    ALU, ACT, AX = mybir.AluOpType, mybir.ActivationFunctionType, mybir.AxisListType

    P = 128
    N, D = x.shape
    T = N // P
    DK = D // P
    HALF = N // 2
    NBLK = 8
    BW = N // NBLK
    BANK = 512
    NB = BW // BANK
    NCH = 4
    CW = BW // NCH
    NF = NCH * 8
    K = 16
    NG = 5
    PLACES = NG * P
    SHORT = 3 * P // 4
    CAP = PLACES - P + SHORT
    PG = 2 * NG
    LW = K + 2
    TW = D + 2
    ONE, E = D, D + 1
    NEG = -1e30
    EPS = 1e-5
    BATCH = 8
    NBATCH = T // BATCH
    NPAIR = BATCH // 2
    QUAD = 4
    LAG = NBATCH - 2
    GB = 8
    EXPMASK, MANT, EBIAS = 0x7F800000, 23, 127

    table = nc.dram_tensor("table", (N, TW), f32, kind="Internal").ap()
    erow = nc.dram_tensor("erow", (T, P), f32, kind="Internal").ap()
    x_b = x.rearrange("(n i p) d -> n p i d", p=P, i=BATCH)
    x_p = x.rearrange("(k t p) d -> k p t d", p=P, t=2)
    out_p = out.rearrange("(k t p) d -> k p t d", p=P, t=2)
    adj_t = adj.rearrange("(t p) (h c) -> t h p c", p=P, h=2)
    table_q = table.rearrange("(q i p) c -> q p i c", p=P, i=QUAD)
    table_g = table.rearrange("(g i p) c -> g p i c", p=P, i=GB)

    with ExitStack() as ctx:
        def sb(name, shape, dt):
            return ctx.enter_context(nc.sbuf_tensor(name, shape, dt))

        def ps(name, shape, dt=f32):
            return ctx.enter_context(nc.psum_tensor(name, shape, dt))

        def sem(name):
            return ctx.enter_context(nc.semaphore(name))

        ident = sb("ident", [P, P], f32)
        shifts = sb("shifts", [P, NBLK, P], bf16)
        ones = sb("ones", [P, P], f32)
        base = sb("base", [P, 2, NF], f32)
        w_sb = sb("w_sb", [P, DK, D], f32)
        bias = sb("bias", [P, D], f32)
        avec = sb("avec", [P, D], f32)
        adj_sb = sb("adj_sb", [P, 2, 2, HALF], i32)
        mask = sb("mask", [P, 2, 2, HALF], bf16)
        halfdeg = sb("halfdeg", [P, 2, T], f32)
        deg = sb("deg", [P, T], f32)
        found = sb("found", [P, T], f32)
        vals = sb("vals", [P, 2, 2, NF], f32)
        pos = sb("pos", [P, 2, NF], u32)
        expo = sb("expo", [P, 2, 2, NF], i32)
        col = sb("col", [P, 2, NF], f32)
        key = sb("key", [P, 2, 2, NF], f32)
        key2 = sb("key2", [P, 2, 2, NF], f32)
        keys = [key2[:, t, :, :].rearrange("p o f -> p (o f)") for t in range(2)]
        top = sb("top", [P, 2, K], f32)
        junk16 = sb("junk16", [P, 2, K], f32)
        lists = sb("lists", [P, T, LW], f32)
        upto = sb("upto", [P, P], f32)
        place = sb("place", [P, PLACES], f32)
        nth = sb("nth", [P, PG, K], f32)
        number = sb("number", [P, P], f32)
        ends = sb("ends", [P, 2], f32)
        begun = sb("begun", [P, 2, PLACES], f32)
        band = sb("band", [P, 2, 2, PLACES], f32)
        which = sb("which", [P, 2, PG, K], f32)
        edge = sb("edge", [P, PG, K], f32)
        ekey = sb("ekey", [P, PG], f32)
        idx = sb("idx", [P, 2, PG], u32)
        owner = sb("owner", [P, 2, PG], f32)
        pen = sb("pen", [P, 2, K], f32)
        which_e = sb("which_e", [P, PG, K], f32)
        sc = sb("sc", [P, 2, K], f32)
        rmax = sb("rmax", [P, 2], f32)
        nmax = sb("nmax", [P, 2], f32)
        arg = sb("arg", [P, PG], f32)
        wt = sb("wt", [P, PG], f32)
        dmax = sb("dmax", [P, 2], f32)
        rden = sb("rden", [P, 2], f32)
        xt = sb("xt", [P, 2, 2, D], f32)
        ot = sb("ot", [P, 2, 2, D], f32)
        xb = sb("xb", [P, 2, PG * TW], f32)
        xrows = xb[:, :, 0:BATCH * D].rearrange("p b (i d) -> p b i d", d=D)
        stats = sb("stats", [P, BATCH, 6], f32)
        msum = sb("msum", [P, BATCH], f32)
        mdif = sb("mdif", [P, BATCH], f32)
        var = sb("var", [P, BATCH], f32)
        std = sb("std", [P, BATCH], f32)
        rstd = sb("rstd", [P, 2, BATCH], f32)
        nmr = sb("nmr", [P, 2, BATCH], f32)
        work = sb("work", [P, 4, 4 * D], f32)
        h, zb, th = [work[:, i, :].rearrange("p (u i d) -> p u i d", u=2, d=D) for i in range(3)]
        hT = work[:, 3, :].rearrange("p (u c) -> p u c", u=2)
        stage = sb("stage", [P, 2, QUAD, TW], f32)
        hsum = sb("hsum", [P, 2, QUAD], f32)
        escore = sb("escore", [P, 2, QUAD], f32)
        epen = sb("epen", [P, 2, QUAD], f32)
        escores = sb("escores", [P, T], f32)
        slots = xb[:, :, :].rearrange("p b (g c) -> p b g c", c=TW)
        work_g = work[:, :, :].rearrange("p b c -> p (b c)")[:, 0:3 * PG * P].rearrange("p (g c) -> p g c", c=P)
        back = [work_g[:, b * PG:(b + 1) * PG, :] for b in range(2)]
        wback = work_g[:, 2 * PG:3 * PG, :]
        lost = sb("lost", [P, 2, T], f32)
        tover = sb("tover", [1, T], f32)
        den = sb("den", [P, 1], f32)
        tord = sb("tord", [1, T], f32)
        tflag = sb("tflag", [1, T], f32)
        tkey = sb("tkey", [1, T], f32)
        tlist = sb("tlist", [1, T], f32)
        tiles = sb("tiles", [1, T], i32)
        nflag = sb("nflag", [1, 1], f32)
        ntiles = sb("ntiles", [1, 1], i32)
        eT = sb("eT", [T, P], f32)

        packed = [[ps(f"packed{p}{n}", [P, BANK]) for n in range(NB)] for p in range(2)]
        pT = [ps(f"pT{p}", [P, BANK]) for p in range(2)]
        pz = [ps(f"pz{p}", [P, BANK]) for p in range(2)]
        acc = pT
        found_at = pz[0][:, 0:PG * LW].rearrange("p (g w) -> p g w", w=LW)
        end = pz[0][:, PG * LW:PG * LW + 2]
        es = pz[1][:, 0:2 * K].rearrange("p (t s) -> p t s", s=K)
        nmax_at = pz[1][:, 2 * K:2 * K + PG]

        consts = sem("consts")
        gconst = sem("gconst")
        params_in = sem("params_in")
        x_in = [sem(f"x_in{p}") for p in range(2)]
        var_ready = sem("var_ready")
        std_ready = sem("std_ready")
        rstd_ready = sem("rstd_ready")
        h_ready = [sem(f"h_ready{p}") for p in range(2)]
        hT_psum = [sem(f"hT_psum{p}") for p in range(2)]
        hT_ready = [sem(f"hT_ready{p}") for p in range(2)]
        z_psum = [sem(f"z_psum{p}") for p in range(2)]
        z_staged = [sem(f"z_staged{p}") for p in range(2)]
        zb_ready = [sem(f"zb_ready{p}") for p in range(2)]
        th_ready = [sem(f"th_ready{p}") for p in range(2)]
        dotted = [sem(f"dotted{p}") for p in range(2)]
        staged = sem("staged")
        stored = sem("stored")
        stage_free = [sem(f"stage_free{p}") for p in range(2)]
        adj_in = [[sem(f"adj_in{p}{i}") for i in range(2)] for p in range(2)]
        adj_free = [[sem(f"adj_free{p}{i}") for i in range(2)] for p in range(2)]
        mask_free = [[sem(f"mask_free{p}{i}") for i in range(2)] for p in range(2)]
        packed_free = [sem(f"packed_free{p}") for p in range(2)]
        idx_ready = sem("idx_ready")
        cleared = sem("cleared")
        gathering = sem("gathering")
        gathered = [sem(f"gathered{p}") for p in range(2)]
        back_ready = sem("back_ready")
        which_e_ready = sem("which_e_ready")
        es_ready = sem("es_ready")
        nmax_ready = sem("nmax_ready")
        nmax_at_ready = sem("nmax_at_ready")
        arg_ready = sem("arg_ready")
        wt_ready = sem("wt_ready")
        wback_ready = sem("wback_ready")
        acc_ready = sem("acc_ready")
        band_ready = sem("band_ready")
        found_at_ready = sem("found_at_ready")
        end_ready = sem("end_ready")
        xt_in = [sem(f"xt_in{p}") for p in range(2)]
        ot_ready = sem("ot_ready")
        ot_out = [sem(f"ot_out{p}") for p in range(2)]
        lost_ready = sem("lost_ready")
        lost_psum = sem("lost_psum")
        count_ready = sem("count_ready")
        list_ready = sem("list_ready")
        et_psum = sem("et_psum")
        et_ready = sem("et_ready")
        erow_out = sem("erow_out")
        g_adj = sem("g_adj")
        g_e = sem("g_e")
        g_x = sem("g_x")
        g_table = [sem(f"g_table{p}") for p in range(2)]
        g_nmax = sem("g_nmax")
        g_w = sem("g_w")
        g_tr = [sem(f"g_tr{p}") for p in range(2)]
        g_wT = [sem(f"g_wT{p}") for p in range(2)]
        g_mm = [sem(f"g_mm{p}") for p in range(2)]
        g_ot = sem("g_ot")
        g_out = sem("g_out")
        g_stored = sem("g_stored")

        g_mask_i = adj_sb[:, 0, :, :].rearrange("p h c -> p (h c)")
        g_mask_f = g_mask_i.bitcast(f32)
        g_w_f = adj_sb[:, 1, :, :].rearrange("p h c -> p (h c)").bitcast(f32)
        g_tab = [xb[:, p, 0:GB * TW].rearrange("p (i c) -> p i c", c=TW) for p in range(2)]
        g_wTs = [work[:, 2 + p, 0:4 * P] for p in range(2)]
        NL = T // GB
        NQ = T // 4

        NCONST = 9 + NBLK

        block = ctx.enter_context(nc.Block())

        NP = T // 2
        LAST = NP - LAG // 2 - 1

        def steps(engine, step):
            for b in range(2):
                step(0, b)
            with engine.Fori(1, LAST // 2) as c:
                step(c, 0)
                step(c, 1)
            for k in range(LAST // 2 * 2, NP):
                step(k // 2, k % 2, scans=max(0, min(2, LAST + 1 - k)), ahead=min(2, NP - 1 - k))

        def free(m):
            return m + 1

        def ready(m):
            return m + 2

        def free2(n):
            return n + 1

        def ready2(n):
            return n + 3

        def after(c, b):
            return (c, 1) if b == 0 else (c + 1, 0)

        def before(c, b):
            return (c, 0) if b == 1 else (c - 1, 1)

        def use(d, bp, j):
            return NPAIR // 2 * (2 * d + bp) + j // 2, j % 2

        def next_batch(d, bp):
            return (d, 1) if bp == 0 else (d + 1, 0)

        def pair(d, bp, j):
            if j >= NPAIR:
                d, bp = next_batch(d, bp)
                j -= NPAIR
            return None if isinstance(d, int) and d == NBATCH // 2 else (d, bp, j)

        @block.sync
        def _(sp):
            sp.dma_start(w_sb[:, :, :], W.rearrange("(k p) d -> p k d", p=P)).then_inc(params_in, 16)
            sp.dma_start(bias[:, :], b.partition_broadcast(P)).then_inc(params_in, 16)
            sp.dma_start(avec[:, :], a.rearrange("d o -> (o d)").partition_broadcast(P)).then_inc(params_in, 16)
            with sp.Fori(0, T // 2) as k:
                for par in range(2):
                    for i in range(2):
                        sp.wait_ge(adj_free[par][i], free(k))
                        sp.dma_start(adj_sb[:, par, i, :],
                                     adj_t[bass.ds(2 * k + par, 1), i, :, :].rearrange("o p c -> (o p) c"))\
                          .then_inc(adj_in[par][i], 16)

            sp.wait_ge(count_ready, 1)
            count = sp.value_load(ntiles[0:1, 0:1], min_val=0, max_val=T)
            with sp.If(count > 0):
                sp.wait_ge(list_ready, 1)
                for par in range(2):
                    sp.wait_ge(ot_out[par], 16 * (NP // 2))
                sp.wait_ge(et_ready, 1)
                sp.dma_start(erow[:, :], eT[:, :]).then_inc(erow_out, 16)
                sp.wait_ge(erow_out, 16)
                sp.sem_inc(g_stored, 1)
                with sp.Fori(0, count) as r:
                    tile = sp.value_load(tiles[0:1, bass.ds(r, 1)], min_val=0, max_val=T - 1)
                    sp.wait_ge(g_stored, free(r))
                    sp.dma_start(g_mask_i, adj[bass.ds(tile * P, P), :]).then_inc(g_adj, 16)
                    sp.dma_start(g_w_f, erow.rearrange("t p -> (t p)").partition_broadcast(P)).then_inc(g_e, 16)
                    sp.dma_start(xt[:, 0, 0, :], x[bass.ds(tile * P, P), :]).then_inc(g_x, 16)
                    for g in range(NL):
                        if g >= 2:
                            sp.wait_ge(g_mm[1], NQ // 2 * r + g - 1)
                        sp.dma_start(g_tab[g % 2], table_g[g]).then_inc(g_table[g % 2], 16)
                    sp.wait_ge(g_ot, r + 1)
                    sp.dma_start(out[bass.ds(tile * P, P), :], ot[:, 0, 0, :]).then_inc(g_out, 16)
                    sp.wait_ge(g_out, 16 * (r + 1))
                    sp.sem_inc(g_stored, 1)

        @block.gpsimd
        def _(pool):
            for q in range(2):
                pool.sem_inc(stage_free[q], 1)
            nc.gpsimd.memset(ident[:, :], 0.0).then_inc(gconst, 1)
            nc.gpsimd.memset(shifts[:, :, :], 0.0).then_inc(gconst, 1)
            nc.gpsimd.memset(ones[:, :], 1.0).then_inc(gconst, 1)
            nc.gpsimd.memset(stage[:, :, :, ONE], 1.0).then_inc(consts, 1)
            nc.gpsimd.iota(lists[:, :, K + 1], pattern=[[0, T]], base=1, channel_multiplier=1,
                           allow_small_or_imprecise_dtypes=True).then_inc(consts, 1)
            nc.gpsimd.iota(place[:, :], pattern=[[1, PLACES]], base=0, channel_multiplier=0,
                           allow_small_or_imprecise_dtypes=True).then_inc(consts, 1)
            nc.gpsimd.iota(nth[:, :, :].rearrange("p (t g) s -> p t g s", t=2), pattern=[[0, 2], [P, NG], [-1, K]], base=0, channel_multiplier=1,
                           allow_small_or_imprecise_dtypes=True).then_inc(consts, 1)
            nc.gpsimd.iota(number[:, :], pattern=[[1, P]], base=1, channel_multiplier=0,
                           allow_small_or_imprecise_dtypes=True).then_inc(consts, 1)
            nc.gpsimd.iota(base[:, :, :].rearrange("p t (c e) -> p t c e", e=8), pattern=[[0, 2], [-CW, NCH], [0, 8]], base=N + EBIAS * BW,
                           channel_multiplier=0, allow_small_or_imprecise_dtypes=True).then_inc(consts, 1)
            nc.gpsimd.iota(tord[:, :], pattern=[[-1, T]], base=T, channel_multiplier=0,
                           allow_small_or_imprecise_dtypes=True).then_inc(consts, 1)
            pool.wait_ge(gconst, 3)
            nc.gpsimd.affine_select(out=ident[:, :], in_=ident[:, :], compare_op=ALU.not_equal, fill=1.0,
                                    base=0, pattern=[[-1, P]], channel_multiplier=1).then_inc(consts, 1)
            nc.gpsimd.affine_select(out=upto[:, :], in_=ones[:, :], compare_op=ALU.is_ge, fill=0.0,
                                    base=0, pattern=[[1, P]], channel_multiplier=-1).then_inc(consts, 1)
            for j in range(NBLK):
                nc.gpsimd.affine_select(out=shifts[:, j, :], in_=shifts[:, j, :], compare_op=ALU.not_equal,
                                        fill=float(2 ** j), base=0, pattern=[[-1, P]],
                                        channel_multiplier=1).then_inc(consts, 1)
            for n in range(NBATCH):
                for q in range(BATCH // QUAD):
                    g = n * (BATCH // QUAD) + q
                    pool.wait_ge(staged, g + 1)
                    pool.dma_start(table_q[g], stage[:, g % 2, :, :]).then_inc(stored, 16)
                    pool.wait_ge(stored, 16 * (g + 1))
                    pool.sem_inc(stage_free[g % 2], 1)

            for u in range(2):
                pool.wait_ge(h_ready[u], ready(T // 4 - 1))
            nc.gpsimd.memset(slots[:, :, :, :], 0.0).then_inc(cleared, 1)
            pool.wait_ge(cleared, 1)
            last_row = pool.alloc_register("last_row")
            pool.reg_mov(last_row, N - 1)

            def gather(c, b):
                k = 2 * c + b
                pool.wait_ge(idx_ready, k + 1)
                pool.wait_ge(acc_ready, free2(k))
                pool.sem_inc(gathering, 1)
                for g in range(PG):
                    rows = SHORT if g % NG == NG - 1 else P
                    pool.indirect_dma_start(
                        out=slots[0:rows, b, g, :], out_offset=None, in_=table[:, :],
                        in_offset=bass.IndirectOffsetOnAxis(ap=idx[0:rows, b, g:g + 1], axis=0),
                        bounds_check=last_row, oob_is_err=False).then_inc(gathered[b], 16)

            with pool.Fori(0, NP // 2) as c:
                gather(c, 0)
                gather(c, 1)

        @block.scalar
        def _(act):
            for par in range(2):
                act.dma_start(xrows[:, par, :, :], x_b[par]).then_inc(x_in[par], 16)
            for par in range(2):
                for i in range(2):
                    act.sem_inc(adj_free[par][i], 1)

            def scan(k, par, halves=(0, 1)):
                for i in halves:
                    act.wait_ge(adj_in[par][i], 16 * (k + 1))
                    act.wait_ge(mask_free[par][i], free(k))
                    nc.scalar.activation(mask[:, par, i, :], adj_sb[:, par, i, :], ACT.Relu,
                                         accum_out=halfdeg[:, i, bass.ds(2 * k + par, 1)])\
                      .then_inc(adj_free[par][i], 1)

            def relu(d, bp, j):
                m, u = use(d, bp, j)
                act.wait_ge(hT_psum[u], free(m))
                for i in range(2):
                    t = 2 * j + i
                    last = nc.scalar.activation(h[:, u, i, :], xrows[:, bp, t, :], ACT.Relu,
                                                scale=rstd[:, bp, t:t + 1], bias=nmr[:, bp, t:t + 1])
                last.then_inc(h_ready[u], 1)

            def load_batch(d, bp):
                for u in range(2):
                    act.wait_ge(h_ready[u], ready(use(d, bp, NPAIR - 2)[0]))
                act.dma_start(xrows[:, bp, :, :], x_b[bass.ds(2 * d + 2 + bp, 1)].rearrange("o p i d -> (o p) i d"))\
                   .then_inc(x_in[bp], 16)

            def stage_z(d, bp, j):
                m, u = use(d, bp, j)
                q, i = j // 2, 2 * (j % 2)
                act.wait_ge(z_psum[u], ready(m))
                if i == 0:
                    act.wait_ge(stage_free[q], free(2 * d + bp))
                nc.scalar.copy(stage[:, q, i:i + 2, 0:D], pz[u].rearrange("p (i d) -> p i d", d=D))\
                  .then_inc(z_staged[u], 1)

            def tanh(d, bp, j):
                m, u = use(d, bp, j)
                act.wait_ge(zb_ready[u], ready(m))
                act.wait_ge(dotted[u], free(m))
                for i in range(2):
                    t = 2 * (j % 2) + i
                    last = nc.scalar.activation(th[:, u, i, :], zb[:, u, i, :], ACT.Tanh,
                                                accum_out=hsum[:, j // 2, t:t + 1])
                last.then_inc(th_ready[u], 1)

            def root(d, bp):
                act.wait_ge(var_ready, 2 * d + bp + 1)
                nc.scalar.activation(std[:, :], var[:, :], ACT.Sqrt).then_inc(std_ready, 1)

            def project(d, scanning=True):
                for bp in range(2):
                    for j in range(NPAIR):
                        stage_z(d, bp, j)
                        if j == 1 and pair(d, bp, NPAIR):
                            root(*next_batch(d, bp))
                        ahead = pair(d, bp, j + 3)
                        if ahead:
                            if ahead[2] == 0:
                                act.wait_ge(rstd_ready, 2 * ahead[0] + ahead[1] + 1)
                            relu(*ahead)
                        tanh(d, bp, j)
                        if j == 0 and not isinstance(d, int):
                            load_batch(d, bp)
                        if scanning and j % 2 == 1:
                            scan(d + 1, bp, [j // 2])

            for u in range(2):
                act.sem_inc(h_ready[u], 1)
                act.sem_inc(z_staged[u], 1)
                act.sem_inc(th_ready[u], 1)
            root(0, 0)
            act.wait_ge(rstd_ready, 1)
            for j in range(3):
                relu(0, 0, j)
            scan(0, 0)
            scan(0, 1)
            with act.Fori(0, NBATCH // 2 - 1) as d:
                project(d)
            project(NBATCH // 2 - 1, scanning=False)

            def load_x(c, b):
                act.wait_ge(ot_ready, free2(2 * c + b))
                act.dma_start(xt[:, b, :, :], x_p[bass.ds(2 * c + b, 1)].rearrange("o p t d -> (o p) t d"))\
                   .then_inc(xt_in[b], 16)

            def store(c, b):
                act.wait_ge(ot_ready, ready2(2 * c + b))
                act.dma_start(out_p[bass.ds(2 * c + b, 1)].rearrange("o p t d -> (o p) t d"), ot[:, b, :, :])\
                   .then_inc(ot_out[b], 16)

            def step(c, b, scans=2, ahead=2):
                k = 2 * c + b
                first = isinstance(k, int) and k == 0
                if scans == 2:
                    scan(k + LAG // 2 + 1, 0)
                if first:
                    scan(k + LAG // 2 + 1, 1)
                act.wait_ge(arg_ready, k + 1)
                nc.scalar.activation(wt[:, :], arg[:, :], ACT.Exp).then_inc(wt_ready, 1)
                if not first:
                    store(*before(c, b))
                load_x(c, b)
                if scans == 2 and not first:
                    scan(k + LAG // 2 + 1, 1)

            steps(act, step)
            store(NP // 2 - 1, 1)
            for par in range(2):
                act.wait_ge(ot_out[par], 16 * (NP // 2))

            act.wait_ge(count_ready, 1)
            count = act.value_load(ntiles[0:1, 0:1], min_val=0, max_val=T)
            with act.If(count > 0):
                with act.Fori(0, count) as r:
                    act.wait_ge(g_nmax, r + 1)
                    nc.scalar.activation(g_w_f, g_w_f, ACT.Exp, bias=nmax[:, 0:1],
                                         accum_out=den[:, :]).then_inc(g_w, 1)

        @block.tensor
        def _(pe):
            for par in range(2):
                pe.sem_inc(hT_psum[par], 1)
                pe.sem_inc(z_psum[par], 1)
                pe.sem_inc(acc_ready, 1)
                for i in range(2):
                    pe.sem_inc(mask_free[par][i], 1)
            pe.wait_ge(consts, NCONST)
            pe.wait_ge(params_in, 48)

            def pack(k, par, halves=(0, 1)):
                for i in halves:
                    pe.wait_ge(adj_free[par][i], ready(k))
                    if i == 0:
                        pe.wait_ge(packed_free[par], free(k))
                    for j in range(NBLK // 2):
                        for n in range(NB):
                            last = nc.tensor.matmul(packed[par][n][:, :], shifts[:, i * NBLK // 2 + j, :],
                                                    mask[:, par, i, j * BW + n * BANK:j * BW + (n + 1) * BANK],
                                                    start=(i == 0 and j == 0), stop=(i == 1 and j == NBLK // 2 - 1))
                    last.then_inc(mask_free[par][i], 1)

            def turn(d, bp, j):
                m, u = use(d, bp, j)
                pe.wait_ge(h_ready[u], ready(m))
                pe.wait_ge(hT_ready[u], free(m))
                for i in range(2):
                    for c in range(DK):
                        last = nc.tensor.transpose(pT[u][:, i * D + c * P:i * D + (c + 1) * P],
                                                   h[:, u, i, c * P:(c + 1) * P], ident[:, :])
                last.then_inc(hT_psum[u], 1)

            def multiply(d, bp, j):
                m, u = use(d, bp, j)
                pe.wait_ge(hT_ready[u], ready(m))
                pe.wait_ge(z_staged[u], free(m))
                for i in range(2):
                    for c in range(DK):
                        last = nc.tensor.matmul(pz[u][:, i * D:(i + 1) * D],
                                                hT[:, u, i * D + c * P:i * D + (c + 1) * P], w_sb[:, c, :],
                                                start=(c == 0), stop=(c == DK - 1))
                last.then_inc(z_psum[u], 1)

            def project(d, scanning=True):
                for bp in range(2):
                    for j in range(NPAIR):
                        if pair(d, bp, j + 1):
                            multiply(*pair(d, bp, j + 1))
                        if pair(d, bp, j + 3):
                            turn(*pair(d, bp, j + 3))
                        if scanning and j % 2 == 1:
                            pack(*next_batch(d, bp), [j // 2])

            turn(0, 0, 0)
            multiply(0, 0, 0)
            turn(0, 0, 1)
            turn(0, 0, 2)
            pack(0, 0)
            with pe.Fori(0, NBATCH // 2 - 1) as d:
                project(d)
            project(NBATCH // 2 - 1, scanning=False)
            for u in range(2):
                pe.wait_ge(z_staged[u], ready(T // 4 - 1))

            def prefix(k):
                nc.tensor.matmul(end, upto[:, :], found[:, bass.ds(2 * k, 2)], start=True, stop=True)\
                  .then_inc(end_ready, 1)

            def look_up(c, b):
                k = 2 * c + b
                pe.wait_ge(band_ready, k + 1)
                for g in range(PG):
                    t, i = g // NG, g % NG
                    last = nc.tensor.matmul(found_at[:, g, :], band[:, b, t, i * P:(i + 1) * P],
                                            lists[:, bass.ds(2 * k + t, 1), :].rearrange("p o w -> p (o w)"),
                                            start=True, stop=True)
                last.then_inc(found_at_ready, 1)

            def scores_back(c, b):
                pe.wait_ge(back_ready, 2 * c + b + 1)
                pe.wait_ge(which_e_ready, 2 * c + b + 1)
                for g in range(PG):
                    last = nc.tensor.matmul(es[:, g // NG, :], back[b][:, g, :], which_e[:, g, :],
                                            start=(g % NG == 0), stop=(g % NG == NG - 1))
                last.then_inc(es_ready, 1)

            def max_out(c, b):
                pe.wait_ge(nmax_ready, 2 * c + b + 1)
                for g in range(PG):
                    t, i = g // NG, g % NG
                    last = nc.tensor.matmul(nmax_at[:, g:g + 1], band[:, b, t, i * P:(i + 1) * P], nmax[:, t:t + 1],
                                            start=True, stop=True)
                last.then_inc(nmax_at_ready, 1)

            def sum_edges(c, b):
                k = 2 * c + b
                pe.wait_ge(wback_ready, k + 1)
                pe.wait_ge(ot_ready, ready2(k - 1))
                for g in range(PG):
                    last = nc.tensor.matmul(acc[g // NG][:, 0:D + 1], wback[:, g, :], slots[:, b, g, 0:D + 1],
                                            start=(g % NG == 0), stop=(g % NG == NG - 1))
                last.then_inc(acc_ready, 1)

            def step(c, b, scans=2, ahead=2):
                k = 2 * c + b
                packing = scans and not (isinstance(k, int) and k == 0)
                scores_back(c, b)
                if ahead >= 2:
                    prefix(k + 2)
                if packing:
                    pack(k + LAG // 2, 1, [0])
                max_out(c, b)
                if packing:
                    pack(k + LAG // 2, 1, [1])
                if ahead >= 2:
                    look_up(c + 1, b)
                if scans == 2:
                    pack(k + LAG // 2 + 1, 0)
                sum_edges(c, b)

            prefix(0)
            look_up(0, 0)
            pe.wait_ge(idx_ready, 1)
            prefix(1)
            look_up(0, 1)
            pack(LAG // 2, 1)
            steps(pe, step)

            pe.wait_ge(lost_ready, 1)
            nc.tensor.matmul(pz[0][:, 0:2 * T], ones[:, :], lost[:, :, :].rearrange("p a t -> p (a t)"),
                             start=True, stop=True).then_inc(lost_psum, 1)

            pe.wait_ge(count_ready, 1)
            count = pe.value_load(ntiles[0:1, 0:1], min_val=0, max_val=T)
            with pe.If(count > 0):
                nc.tensor.transpose(pz[0][0:T, 0:P], escores[:, :], ident[:, :]).then_inc(et_psum, 1)
                with pe.Fori(0, count) as r:
                    def products(q):
                        pe.wait_ge(g_wT[q % 2], NQ // 2 * r + q // 2 + 1)
                        g = q // 2
                        pe.wait_ge(g_table[g % 2], 16 * (NL // 2 * r + g // 2 + 1))
                        for c in range(4):
                            last = nc.tensor.matmul(acc[0][:, 0:D], g_wTs[q % 2][:, c * P:(c + 1) * P],
                                                    g_tab[g % 2][:, 4 * (q % 2) + c, 0:D],
                                                    start=(q == 0 and c == 0), stop=(q == NQ - 1 and c == 3))
                        last.then_inc(g_mm[q % 2], 1)
                        return last

                    pe.wait_ge(g_w, r + 1)
                    for q in range(NQ):
                        if q >= 2:
                            pe.wait_ge(g_wT[q % 2], NQ // 2 * r + q // 2)
                        for c in range(4):
                            last = nc.tensor.transpose(packed[q % 2][0][:, c * P:(c + 1) * P],
                                                       g_w_f[:, (4 * q + c) * P:(4 * q + c + 1) * P], ident[:, :])
                        last.then_inc(g_tr[q % 2], 1)
                        if q >= 1:
                            products(q - 1)
                    products(NQ - 1)

        @block.vector
        def _(dve):
            for par in range(2):
                dve.sem_inc(packed_free[par], 1)
                dve.sem_inc(hT_ready[par], 1)
                dve.sem_inc(zb_ready[par], 1)
                dve.sem_inc(dotted[par], 1)
                dve.sem_inc(ot_ready, 1)
            dve.wait_ge(consts, NCONST)
            dve.wait_ge(params_in, 48)

            v = nc.vector

            def find(k, par):
                dve.wait_ge(mask_free[par][1], ready(k))
                v.tensor_tensor(deg[:, bass.ds(2 * k + par, 1)], halfdeg[:, 0, bass.ds(2 * k + par, 1)],
                                halfdeg[:, 1, bass.ds(2 * k + par, 1)], op=ALU.add)
                chunks = [packed[par][c * CW // BANK][:, c * CW % BANK:c * CW % BANK + CW] for c in range(NCH)]
                for c in range(NCH):
                    v.max(out=vals[:, 0, par, 8 * c:8 * c + 8], in_=chunks[c])
                v.drain()
                for c in range(NCH):
                    last = v.max_index(out=pos[:, par, 8 * c:8 * c + 8], in_max=vals[:, 0, par, 8 * c:8 * c + 8],
                                       in_values=chunks[c])
                last.then_inc(packed_free[par], 1)

            def collect(k):
                v.drain()
                v.tensor_single_scalar(expo[:, 0, :, :], vals[:, 0, :, :].bitcast(i32), EXPMASK, op=ALU.bitwise_and)
                v.tensor_tensor(col[:, :, :], base[:, :, :], pos[:, :, :], op=ALU.subtract)
                v.drain()
                v.tensor_tensor(vals[:, 1, :, :], vals[:, 0, :, :], expo[:, 0, :, :].bitcast(f32), op=ALU.subtract)
                v.drain()
                v.tensor_single_scalar(expo[:, :, :, :].rearrange("p o t f -> p (o t f)"),
                                       vals[:, :, :, :].rearrange("p o t f -> p (o t f)").bitcast(i32),
                                       MANT, op=ALU.logical_shift_right)
                v.drain()
                for o in range(2):
                    v.scalar_tensor_tensor(key[:, :, o, :], in0=expo[:, o, :, :], scalar=-float(BW), in1=col[:, :, :],
                                           op0=ALU.mult, op1=ALU.add)
                v.drain()
                for o in range(2):
                    v.scalar_tensor_tensor(key2[:, :, o, :], in0=vals[:, o, :, :], scalar=0.0, in1=key[:, :, o, :],
                                           op0=ALU.is_gt, op1=ALU.mult)
                v.drain()
                for t in range(2):
                    v.max(out=top[:, t, 0:8], in_=keys[t])
                v.drain()
                for t in range(2):
                    v.match_replace(out=keys[t], in_to_replace=top[:, t, 0:8], in_values=keys[t], imm_value=0.0)
                v.drain()
                for t in range(2):
                    v.max(out=top[:, t, 8:16], in_=keys[t])
                v.drain()
                v.tensor_scalar(junk16[:, :, :], top[:, :, :], 0.0, None, op0=ALU.is_gt)
                v.tensor_scalar(lists[:, bass.ds(2 * k, 2), 0:K], top[:, :, :], 1.0, None, op0=ALU.mult)
                v.drain()
                v.tensor_reduce(found[:, bass.ds(2 * k, 2)], junk16[:, :, :], axis=AX.X, op=ALU.add)
                v.drain()

            def statistics(d, bp, tiles):
                for i in tiles:
                    if i == 0:
                        dve.wait_ge(x_in[bp], 16 * (d + 1))
                    v.bn_stats(out=stats[:, i, :], in_=xrows[:, bp, i, :])

            def variance():
                v.drain()
                v.tensor_tensor(msum[:, :], stats[:, :, 1], stats[:, :, 4], op=ALU.add)
                v.tensor_tensor(mdif[:, :], stats[:, :, 1], stats[:, :, 4], op=ALU.subtract)
                v.tensor_tensor(var[:, :], stats[:, :, 2], stats[:, :, 5], op=ALU.add)
                v.drain()
                v.scalar_tensor_tensor(mdif[:, :], in0=mdif[:, :], scalar=0.25, in1=mdif[:, :],
                                       op0=ALU.mult, op1=ALU.mult)
                v.tensor_scalar(var[:, :], var[:, :], 1.0 / D, EPS, op0=ALU.mult, op1=ALU.add)
                v.drain()
                v.tensor_tensor(var[:, :], var[:, :], mdif[:, :], op=ALU.add).then_inc(var_ready, 1)

            def normaliser(d, bp):
                dve.wait_ge(std_ready, 2 * d + bp + 1)
                v.reciprocal(rstd[:, bp, :], std[:, :])
                v.drain()
                v.scalar_tensor_tensor(nmr[:, bp, :], in0=msum[:, :], scalar=-0.5, in1=rstd[:, bp, :],
                                       op0=ALU.mult, op1=ALU.mult).then_inc(rstd_ready, 1)

            def copy_hT(d, bp, j):
                m, u = use(d, bp, j)
                dve.wait_ge(hT_psum[u], ready(m))
                dve.wait_ge(z_psum[u], free(m))
                v.tensor_copy(hT[:, u, :], pT[u][:, :]).then_inc(hT_ready[u], 1)

            def add_bias(d, bp, j):
                m, u = use(d, bp, j)
                q, i = j // 2, 2 * (j % 2)
                dve.wait_ge(z_staged[u], ready(m))
                dve.wait_ge(th_ready[u], free(m))
                v.tensor_tensor(zb[:, u, :, :], stage[:, q, i:i + 2, 0:D],
                                bias[:, :].unsqueeze(1).broadcast_to([P, 2, D]), op=ALU.add)\
                 .then_inc(zb_ready[u], 1)

            def dot_a(d, bp, j):
                m, u = use(d, bp, j)
                dve.wait_ge(th_ready[u], ready(m))
                for i in range(2):
                    t = 2 * (j % 2) + i
                    last = v.scalar_tensor_tensor(th[:, u, i, :], in0=th[:, u, i, :], scalar=1.0, in1=avec[:, :],
                                                  op0=ALU.mult, op1=ALU.mult,
                                                  accum_out=escore[:, j // 2, t:t + 1])
                last.then_inc(dotted[u], 1)

            def scores(d, bp, q):
                g = 2 * (2 * d + bp) + q
                v.drain()
                v.tensor_scalar(epen[:, q, :], hsum[:, q, :], 0.0, NEG, op0=ALU.is_equal, op1=ALU.mult)
                v.drain()
                v.tensor_tensor(escores[:, bass.ds(QUAD * g, QUAD)], escore[:, q, :], epen[:, q, :], op=ALU.add)
                v.tensor_tensor(stage[:, q, :, E], escore[:, q, :], epen[:, q, :], op=ALU.add).then_inc(staged, 1)

            def project(d, scanning=True):
                for bp in range(2):
                    for j in range(NPAIR):
                        if j == 1 and pair(d, bp, NPAIR):
                            normaliser(*next_batch(d, bp))
                        if pair(d, bp, j + 2):
                            copy_hT(*pair(d, bp, j + 2))
                        add_bias(d, bp, j)
                        if j == 0 and pair(d, bp, NPAIR):
                            statistics(*next_batch(d, bp), range(BATCH // 2, BATCH))
                            variance()
                        if j == 3 and not isinstance(d, int):
                            statistics(d + 1, bp, range(BATCH // 2))
                        dot_a(d, bp, j)
                        if j % 2 == 1:
                            scores(d, bp, j // 2)
                        if scanning and j == 1:
                            find(d, bp)
                    if scanning and bp == 1:
                        collect(d)

            statistics(0, 0, range(BATCH))
            variance()
            normaliser(0, 0)
            copy_hT(0, 0, 0)
            copy_hT(0, 0, 1)
            statistics(0, 1, range(BATCH // 2))
            with dve.Fori(0, NBATCH // 2 - 1) as d:
                project(d)
            project(NBATCH // 2 - 1, scanning=False)

            def select(c, b):
                dve.wait_ge(found_at_ready, 2 * c + b + 1)
                v.tensor_tensor(which[:, b, :, :], nth[:, :, :], found_at[:, :, K:K + 1].broadcast_to([P, PG, K]),
                                op=ALU.is_equal)
                v.tensor_copy(owner[:, b, :], found_at[:, :, K + 1])
                v.drain()
                v.tensor_tensor(edge[:, :, :], which[:, b, :, :], found_at[:, :, 0:K], op=ALU.mult)
                v.drain()
                v.tensor_reduce(ekey[:, :], edge[:, :, :], axis=AX.X, op=ALU.add)
                v.drain()
                v.tensor_scalar(idx[:, b, :], ekey[:, :], -1.0, float(N), op0=ALU.mult, op1=ALU.add)\
                 .then_inc(idx_ready, 1)

            def edge_rows(c, b):
                v.tensor_tensor(back[b], number[:, :].unsqueeze(1).broadcast_to([P, PG, P]),
                                owner[:, b, :].unsqueeze(2).broadcast_to([P, PG, P]), op=ALU.is_equal)\
                 .then_inc(back_ready, 1)

            def score_edges(c, b):
                dve.wait_ge(gathered[b], 16 * PG * (c + 1))
                v.tensor_tensor(which_e[:, :, :], which[:, b, :, :],
                                slots[:, b, :, E:E + 1].broadcast_to([P, PG, K]), op=ALU.mult)\
                 .then_inc(which_e_ready, 1)
                v.tensor_scalar(pen[:, :, :], lists[:, bass.ds(4 * c + 2 * b, 2), 0:K], 0.0, NEG,
                                op0=ALU.is_equal, op1=ALU.mult)
                v.drain()

            def row_max(c, b):
                dve.wait_ge(es_ready, 2 * c + b + 1)
                v.tensor_tensor(sc[:, :, :], es, pen[:, :, :], op=ALU.add)
                v.drain()
                v.tensor_reduce(rmax[:, :], sc[:, :, :], axis=AX.X, op=ALU.max)
                v.drain()
                v.tensor_scalar(nmax[:, :], rmax[:, :], -1.0, -NEG / 10, op0=ALU.mult, op1=ALU.min)\
                 .then_inc(nmax_ready, 1)

            def bounds(c, b):
                k = 2 * c + b
                dve.wait_ge(end_ready, k + 1)
                v.tensor_tensor(lists[:, bass.ds(2 * k, 2), K], end, found[:, bass.ds(2 * k, 2)], op=ALU.subtract)
                v.tensor_copy(ends[:, :], end)
                v.drain()
                for t in range(2):
                    v.tensor_scalar(begun[:, t, :], place[:, :], lists[:, bass.ds(2 * k + t, 1), K], None,
                                    op0=ALU.is_ge)
                v.drain()

            def less_max(c, b):
                dve.wait_ge(nmax_at_ready, 2 * c + b + 1)
                v.tensor_tensor(arg[:, :], slots[:, b, :, E], nmax_at, op=ALU.add)
                v.drain()
                v.tensor_scalar(arg[:, :], arg[:, :], 1.0, None, op0=ALU.min).then_inc(arg_ready, 1)

            def lay_out(b):
                for t in range(2):
                    last = v.scalar_tensor_tensor(band[:, b, t, :], in0=place[:, :], scalar=ends[:, t:t + 1],
                                                  in1=begun[:, t, :], op0=ALU.is_lt, op1=ALU.mult)
                last.then_inc(band_ready, 1)

            def weigh(c, b):
                dve.wait_ge(wt_ready, 2 * c + b + 1)
                v.tensor_tensor(wback, back[b], wt[:, :].unsqueeze(2).broadcast_to([P, PG, P]), op=ALU.mult)\
                 .then_inc(wback_ready, 1)

            def finish(c, b):
                dve.wait_ge(acc_ready, ready2(2 * c + b))
                for t in range(2):
                    v.tensor_scalar(dmax[:, t:t + 1], acc[t][:, D:D + 1], 1e-30, None, op0=ALU.max)
                v.drain()
                v.reciprocal(rden[:, :], dmax[:, :])
                v.drain()
                dve.wait_ge(xt_in[b], 16 * (c + 1))
                if not (isinstance(c, int) and c == 0):
                    dve.wait_ge(ot_out[b], 16 * c)
                for t in range(2):
                    last = v.scalar_tensor_tensor(ot[:, b, t, :], in0=acc[t][:, 0:D], scalar=rden[:, t:t + 1],
                                                  in1=xt[:, b, t, :], op0=ALU.mult, op1=ALU.add)
                last.then_inc(ot_ready, 1)

            def step(c, b, scans=2, ahead=2):
                k = 2 * c + b
                if ahead >= 1:
                    select(*after(c, b))
                score_edges(c, b)
                if scans:
                    find(k + LAG // 2, 0)
                if not (isinstance(k, int) and k == 0):
                    finish(*before(c, b))
                row_max(c, b)
                if ahead >= 2:
                    bounds(c + 1, b)
                less_max(c, b)
                if ahead >= 2:
                    lay_out(b)
                if scans:
                    find(k + LAG // 2, 1)
                if ahead >= 1:
                    edge_rows(*after(c, b))
                weigh(c, b)
                if scans:
                    collect(k + LAG // 2)

            for b in range(2):
                bounds(0, b)
                lay_out(b)
                if b == 0:
                    select(0, 0)
                    edge_rows(0, 0)
            steps(dve, step)
            v.tensor_copy(lost[:, 1, :], found[:, :])
            v.tensor_tensor(lost[:, 0, :], deg[:, :], found[:, :], op=ALU.subtract).then_inc(lost_ready, 1)
            finish(NP // 2 - 1, 1)

            dve.wait_ge(lost_psum, 1)
            v.tensor_scalar(tover[:, :], pz[0][0:1, T:2 * T], float(CAP), None, op0=ALU.is_gt)
            v.drain()
            v.scalar_tensor_tensor(tflag[:, :], in0=pz[0][0:1, 0:T], scalar=0.0, in1=tover[:, :],
                                   op0=ALU.is_gt, op1=ALU.max)
            v.drain()
            v.tensor_reduce(nflag[:, :], tflag[:, :], axis=AX.X, op=ALU.add)
            v.drain()
            v.tensor_copy(ntiles[:, :], nflag[:, :]).then_inc(count_ready, 1)

            dve.wait_ge(count_ready, 1)
            count = dve.value_load(ntiles[0:1, 0:1], min_val=0, max_val=T)
            with dve.If(count > 0):
                v.tensor_tensor(tkey[:, :], tflag[:, :], tord[:, :], op=ALU.mult)
                v.drain()
                for g in range(T // 8):
                    v.max(out=tlist[:, 8 * g:8 * g + 8], in_=tkey[:, :])
                    v.drain()
                    v.match_replace(out=tkey[:, :], in_to_replace=tlist[:, 8 * g:8 * g + 8],
                                    in_values=tkey[:, :], imm_value=0.0)
                    v.drain()
                v.tensor_scalar(tiles[:, :], tlist[:, :], -1.0, float(T), op0=ALU.mult, op1=ALU.add)\
                 .then_inc(list_ready, 1)
                dve.wait_ge(et_psum, 1)
                v.tensor_copy(eT[:, :], pz[0][0:T, 0:P]).then_inc(et_ready, 1)
                with dve.Fori(0, count) as r:
                    dve.wait_ge(g_adj, 16 * (r + 1))
                    v.tensor_scalar(g_mask_f, g_mask_i, 0.0, NEG, op0=ALU.is_le, op1=ALU.mult)
                    v.drain()
                    dve.wait_ge(g_e, 16 * (r + 1))
                    v.tensor_tensor(g_w_f, g_w_f, g_mask_f, op=ALU.add)
                    v.drain()
                    v.tensor_reduce(rmax[:, 0:1], g_w_f, axis=AX.X, op=ALU.max)
                    v.drain()
                    v.tensor_scalar(nmax[:, 0:1], rmax[:, 0:1], -1.0, -NEG / 10, op0=ALU.mult, op1=ALU.min)\
                     .then_inc(g_nmax, 1)
                    dve.wait_ge(g_w, r + 1)
                    v.tensor_scalar(dmax[:, 0:1], den[:, :], 1e-30, None, op0=ALU.max)
                    v.drain()
                    v.reciprocal(rden[:, 0:1], dmax[:, 0:1])
                    for q in range(NQ):
                        dve.wait_ge(g_tr[q % 2], NQ // 2 * r + q // 2 + 1)
                        if q >= 2:
                            dve.wait_ge(g_mm[q % 2], NQ // 2 * r + q // 2)
                        v.tensor_copy(g_wTs[q % 2], packed[q % 2][0][:, :]).then_inc(g_wT[q % 2], 1)
                    dve.wait_ge(g_mm[1], NQ // 2 * (r + 1))
                    dve.wait_ge(g_x, 16 * (r + 1))
                    v.scalar_tensor_tensor(ot[:, 0, 0, :], in0=acc[0][:, 0:D], scalar=rden[:, 0:1], in1=xt[:, 0, 0, :],
                                           op0=ALU.mult, op1=ALU.add).then_inc(g_ot, 1)


_INS = ['x', 'adj', 'L0_gnn_W', 'L0_gnn_b', 'L0_gnn_a']


def kernel(**inputs):
    import numpy as _np
    import concourse.bacc as _bacc
    from concourse import mybir as _mybir
    from concourse.bass_utils import run_bass_kernel_spmd as _run

    nc = _bacc.Bacc("TRN2", target_bir_lowering=False, num_devices=1)
    arrays, args = {}, []
    for name in _INS:
        v = _np.ascontiguousarray(inputs[name])
        arrays[f"in_{name}_dram"] = v
        args.append(nc.dram_tensor(f"in_{name}_dram", v.shape, _mybir.dt.from_np(v.dtype), kind="ExternalInput").ap())
    out = nc.dram_tensor("out_dram", args[0].shape, _mybir.dt.float32, kind="ExternalOutput").ap()
    gnn_layer(nc, *args, out)
    return _run(nc, [arrays], core_ids=[0]).results[0]["out_dram"]
```
